# Optimizing a Trainium2 kernel written in Bass

```python
import numpy as np
import jax
import jax.numpy as jnp

def _softmax(x, axis=-1):
    return jax.nn.softmax(x, axis=axis)

def _gelu(x):
    return jax.nn.gelu(x, approximate=True)

def _silu(x):
    return jax.nn.silu(x)

def _sigmoid(x):
    return jax.nn.sigmoid(x)

def _layernorm(x, axis=-1, eps=1e-05):
    m = jnp.mean(x, axis=axis, keepdims=True)
    v = jnp.var(x, axis=axis, keepdims=True)
    return (x - m) / jnp.sqrt(v + eps)

def _scatter_add(tgt, idx, src, axis=0):
    return tgt.at[idx].add(src)

def _segment_sum(src, seg, n):
    return jax.ops.segment_sum(src, seg, n)
kernel_name = 'mk_adj_ffn_d1_adj_r2_484092'

def setup_inputs(seed: int=0):
    np.random.seed(seed)
    _w = jnp.asarray

    def _rec_inputs():
        import jax
        import jax.numpy as jnp
        _gk = jax.random.key(seed)
        x = -8.776e-05 + 1 * jax.random.normal(jax.random.fold_in(_gk, 1), (2048, 256), jnp.float32)
        _a = jax.random.bernoulli(jax.random.fold_in(_gk, 2), 0.0078125, (2048, 2048))
        _a = jnp.logical_or(_a, jnp.swapaxes(_a, -1, -2))
        _a = jnp.logical_or(_a, jnp.eye(2048, dtype=bool))
        _af = _a.astype(jnp.float32)
        _af = _af * jax.random.uniform(jax.random.fold_in(_gk, 3), (2048, 2048), jnp.float32, 0.05, 1)
        adj = _af
        return (x, adj)
    x, adj = _rec_inputs()

    def _L0_gnn_setup():
        import jax, jax.numpy as jnp
        import numpy as np
        N, NFEAT, NHID = (5000, 256, 256)
        key = jax.random.key(seed)
        ks = jax.random.split(key, 8)
        x = jax.random.normal(ks[0], (N, NFEAT), dtype=jnp.float32)
        adj = jax.random.uniform(ks[1], (N, N), dtype=jnp.float32)
        s = 1.0 / np.sqrt(NFEAT)
        W1 = jax.random.uniform(ks[2], (NFEAT, NHID), jnp.float32, -s, s)
        b1 = jax.random.uniform(ks[3], (NHID,), jnp.float32, -s, s)
        sh = 1.0 / np.sqrt(NHID)
        W3 = jax.random.uniform(ks[4], (NHID, NHID), jnp.float32, -sh, sh)
        b3 = jax.random.uniform(ks[5], (NHID,), jnp.float32, -sh, sh)
        Wf = jax.random.uniform(ks[6], (NHID, NHID), jnp.float32, -sh, sh)
        bf = jax.random.uniform(ks[7], (NHID,), jnp.float32, -sh, sh)
        return {'x': x, 'adj': adj, 'W1': W1, 'b1': b1, 'W3': W3, 'b3': b3, 'Wf': Wf, 'bf': bf}
    _L0_gnn_all = _L0_gnn_setup()
    _L0_gnn_in = {k: v for k, v in _L0_gnn_all.items() if k in ('W1', 'b1', 'W3', 'b3', 'Wf', 'bf')}
    del _L0_gnn_all

    def _L0_ffn_setup():
        import jax, jax.numpy as jnp
        import numpy as np
        D = 256
        H = 1024
        E = 8
        TOPK = 2
        key = jax.random.key(seed)
        ks = jax.random.split(key, 5)
        s = 0.02
        x = jax.random.normal(ks[0], (4, 4096, D), dtype=jnp.float32)
        gate_w = jax.random.normal(ks[1], (D, E), dtype=jnp.float32) * s
        W1 = jax.random.normal(ks[2], (E, D, H), dtype=jnp.float32) * s
        W3 = jax.random.normal(ks[3], (E, D, H), dtype=jnp.float32) * s
        W2 = jax.random.normal(ks[4], (E, H, D), dtype=jnp.float32) * s
        return {'x': x, 'gate_w': gate_w, 'W1': W1, 'W2': W2, 'W3': W3}
    _L0_ffn_all = _L0_ffn_setup()
    _L0_ffn_in = {k: v for k, v in _L0_ffn_all.items() if k in ('gate_w', 'W1', 'W2', 'W3')}
    del _L0_ffn_all
    return {'x': x, 'adj': adj, 'L0_gnn_W1': _L0_gnn_in['W1'], 'L0_gnn_b1': _L0_gnn_in['b1'], 'L0_gnn_W3': _L0_gnn_in['W3'], 'L0_gnn_b3': _L0_gnn_in['b3'], 'L0_gnn_Wf': _L0_gnn_in['Wf'], 'L0_gnn_bf': _L0_gnn_in['bf'], 'L0_ffn_gate_w': _L0_ffn_in['gate_w'], 'L0_ffn_W1': _L0_ffn_in['W1'], 'L0_ffn_W2': _L0_ffn_in['W2'], 'L0_ffn_W3': _L0_ffn_in['W3']}

def reference(x, adj, L0_gnn_W1, L0_gnn_b1, L0_gnn_W3, L0_gnn_b3, L0_gnn_Wf, L0_gnn_bf, L0_ffn_gate_w, L0_ffn_W1, L0_ffn_W2, L0_ffn_W3):
    import jax
    import jax.numpy as jnp

    def _L0_gnn_ref(x, adj, W1, b1, W3, b3, Wf, bf):
        import jax, jax.numpy as jnp
        import numpy as np
        N, NFEAT, NHID = (5000, 256, 256)
        h = jax.nn.relu(adj @ (x @ W1) + b1)
        h = jax.nn.relu(adj @ (h @ W3) + b3)
        return jnp.tanh(h @ Wf + bf)

    def _L0_ffn_ref(x, gate_w, W1, W2, W3):
        import jax, jax.numpy as jnp
        import numpy as np
        D = 256
        H = 1024
        E = 8
        TOPK = 2
        B, S, _ = x.shape
        xt = x.reshape(-1, D)
        T = xt.shape[0]
        gate_logits = xt @ gate_w
        w, idx = jax.lax.top_k(gate_logits, TOPK)
        w = jax.nn.softmax(w, axis=1).astype(xt.dtype)
        comb = jnp.zeros((T, E), dtype=xt.dtype).at[jnp.arange(T)[:, None], idx].add(w)
        out = jnp.zeros_like(xt)
        for e in range(E):
            h = jax.nn.silu(xt @ W1[e]) * (xt @ W3[e])
            out = out + h @ W2[e] * comb[:, e:e + 1]
        return out.reshape(B, S, D)
    x = x + _L0_gnn_ref(_layernorm(x, axis=-1), adj, L0_gnn_W1, L0_gnn_b1, L0_gnn_W3, L0_gnn_b3, L0_gnn_Wf, L0_gnn_bf)
    x = x + _L0_ffn_ref(_layernorm(x, axis=-1)[None], L0_ffn_gate_w, L0_ffn_W1, L0_ffn_W2, L0_ffn_W3)[0]
    return x

_drawn_inputs = setup_inputs


def setup_inputs(seed=0):
    import zlib

    import numpy as np

    out = dict(_drawn_inputs(seed))
    spreads = {}
    factors = {'L0_gnn_b1': 2.864,
     'L0_gnn_b3': 8.0,
     'L0_gnn_bf': 5.287,
     'L0_ffn_gate_w': 3.53,
     'L0_ffn_W1': 3.215,
     'L0_ffn_W2': 3.12,
     'L0_ffn_W3': 3.107}
    for name, (base, spread) in spreads.items():
        noise = np.random.default_rng([zlib.crc32(name.encode()), seed]).standard_normal(out[name].shape)
        drawn = base * np.exp(spread * noise) if base else spread * noise
        out[name] = jnp.asarray(drawn.astype(out[name].dtype))
    for name, factor in factors.items():
        out[name] = (out[name] * factor).astype(out[name].dtype)
    return out
```

```python
import concourse.bass as bass
from concourse import mybir
from concourse.alu_op_type import AluOpType as ALU
from contextlib import ExitStack

F32 = mybir.dt.float32
F32R = mybir.dt.float32r
BF16 = mybir.dt.bfloat16
I32 = mybir.dt.int32
U32 = mybir.dt.uint32
ACT = mybir.ActivationFunctionType
AX = mybir.AxisListType


def gnn_and_routed_ffn(nc, x, adj, W1, b1, W3, b3, Wf, bf, gate_w, EW1, EW2, EW3, out):
    P = nc.NUM_PARTITIONS
    N, D = x.shape
    E, _, H = EW1.shape
    KD = D // P
    KH = H // P
    NT = N // P
    CT = 4
    NC = NT // CT
    CW = CT * P
    TOPK = 2
    TILES = (TOPK * N + E * (P - 1)) // P
    EPS = 1e-5
    HW = 512
    RING = 3
    YR = 3
    assert TILES % YR == 0 and NT * E == P and KD == 2

    table = nc.dram_tensor("ffn_in_rows", (N + P, D), F32).ap()

    ctx = ExitStack()
    with ctx:
        def sem(name):
            return ctx.enter_context(nc.semaphore(name))

        KB = 1024
        arena = ctx.enter_context(nc.sbuf_tensor("arena", [P, 202 * KB // 4], F32))
        base = 16512

        def at(name, shape, dtype, kb):
            return nc.alloc_sbuf_tensor_at(name, shape, dtype, offset=base + int(kb * KB))

        adj_s = at("adj_s", [P, NT, N], F32, 0)
        x_in = at("x_in", [P, NT, D], F32, 112)
        Z = at("Z", [P, 2, NT, D], F32R, 128)
        z2 = at("z2", [P, NT, D], F32, 160)
        x_res = at("x_res", [P, CT, D], F32, 160)
        x1 = at("x1", [P, CT, D], F32, 164)
        xn1 = x_res
        xT = at("xT", [P, 2, KD, P], F32, 168)
        oh_q = at("oh_q", [P, 2, P], F32R, 172)
        oh_s = at("oh_s", [P, 2, 3 * P], F32R, 173)
        zero_rows = at("zero_rows", [P, D], F32, 176)
        hT = at("hT", [P, 2, KD, CW], F32, 176)
        ring = at("ring", [P, RING, 2, CW], F32R, 184)
        Wg = at("Wg", [P, 3, KD, D], F32, 196)
        route = at("route", [P, KB // 2], F32, 196)
        w_raw = at("w_raw", [P, 3, 2 * H], F32, 0)
        EWS = 12 * H
        ew = at("ew", [P, 2 * EWS], F32R, 24)
        xg = at("xg", [P, TILES, D], F32, 120)
        heT = at("heT", [P, 2, KH, P], F32R, 160)
        he = at("he", [P, H], F32, 168)
        sil = at("sil", [P, 2, HW], F32, 172)
        y_st = at("y_st", [P, YR, D], F32, 176)
        xs = at("xs", [P, D], F32, 179)
        xeT = at("xeT", [P, 2, KD, P], F32R, 184)

        def sb(name, shape, dt):
            return ctx.enter_context(nc.sbuf_tensor(name, shape, dt))

        ident = sb("ident", [P, P], F32)
        iota = sb("iota", [P, P], F32)
        tri = sb("tri", [P, P], BF16)
        ones_b = sb("ones_b", [P, P], BF16)
        bf_row = sb("bf_row", [1, D], F32)
        one_row = sb("one_row", [1, P], F32)
        gw = sb("gw", [P, KD, E], F32)
        bT = sb("bT", [P, 2, KD], F32)
        m_run = sb("m_run", [P, CT + 1, E], F32)
        pcol = sb("pcol", [P, 1], F32)
        idx = sb("idx", [P, TILES], I32)
        wt = sb("wt", [P, TILES], F32)
        idx_st = sb("idx_st", [P, YR, 1], I32)

        used = [0]

        def cut(*shape):
            n = 1
            for s in shape:
                n *= s
            v = route[:, used[0]:used[0] + n]
            used[0] += n
            if len(shape) == 1:
                return v
            names = " ".join("abcd"[:len(shape)])
            return v.rearrange(f"p ({names}) -> p {names}", **dict(zip("abcd", shape)))

        stats = sb("stats", [P, CT, 6], F32)
        mv = sb("mv", [P, CT, 2], F32)
        std = sb("std", [P, CT], F32)
        rstd = sb("rstd", [P, CT], F32)
        m8 = cut(CT, E)
        ix8 = cut(CT, E).bitcast(U32)
        oh = cut(2, CT, E)
        ohpos = cut(2, CT, E)
        idxf = cut(2, CT)
        dlt = cut(CT)
        ex = cut(CT)
        wk = cut(2, CT)
        gsl = cut(2 * CT).bitcast(I32)
        qi = cut(2 * CT).bitcast(I32)
        si = cut(2 * CT).bitcast(I32)
        qf = cut(2 * CT)
        sf = cut(2 * CT)
        posk = cut(2, CT)
        cnt = cut(E)
        cnt_i = cut(E).bitcast(I32)
        tl = cut(2, E)
        end = cut(E)
        sq = cut(2)
        vcol = sb("vcol", [P, NT], F32)
        eq_q = sb("eq_q", [P, E], F32)
        kq = sb("kq", [P, 1], F32)
        m_bf = sb("m_bf", [P, 2, CT * E], BF16)
        whi = sb("whi", [P, 2, 2 * CT], F32R)
        info = at("info", [P, 2, P], F32, 184)
        sel = at("sel", [P, P], F32, 185)
        tmp_j = at("tmp_j", [P, 8 * P], F32, 186)
        te_i = sb("te_i", [1, 2, TILES], I32)

        bank = [ctx.enter_context(nc.psum_tensor(f"bank{i}", [P, HW], F32)) for i in range(8)]
        acc = [[bank[0], bank[1]], [bank[2], bank[3]]]
        tp = [bank[4], bank[5]]
        sm = [bank[6], bank[7]]
        xn_p = [bank[4], bank[7]]
        info_p = bank[5]
        gate_p = sm[0][:, 256:256 + CT * E]
        pos_p = sm[1][:, 256:256 + CT * E]
        cnt_p = sm[1][:, 320:320 + E]
        sel_p = sm[0][:, 320:320 + 2 * TILES].rearrange("p (a j) -> p a j", a=2)
        up_p = bank[0:4]
        heT_p = bank[4:6]
        y_p = bank[6]
        xe_p = bank[7]

        s_const = sem("s_const")
        s_zero = sem("s_zero")
        s_x = [sem(f"s_x_in{g}") for g in range(NC)]
        s_w = sem("s_w")
        s_adj = [sem("s_adj_even"), sem("s_adj_odd")]
        s_pool = sem("s_pool_own")
        s_alone = sem("s_alone")
        s_dve = sem("s_dve_own")
        s_sqrt = sem("s_sqrt")
        s_var = sem("s_var")
        s_xn = sem("s_xn")
        s_xtp = sem("s_xT_psum")
        s_xt = sem("s_xT")
        s_zp = sem("s_z_psum")
        s_zhi = sem("s_z_hi")
        s_zlo = sem("s_z_lo")
        s_tp = sem("s_adjT_psum")
        s_hi = sem("s_ring_hi")
        s_lo = sem("s_ring_lo")
        s_adjT = sem("s_adjT")
        s_mm = sem("s_adj_products")
        s_h = sem("s_hT")
        s_z2p = sem("s_z2_psum")
        s_z2 = sem("s_z2")
        s_up = sem("s_u_psum")
        s_th = sem("s_tanh")
        s_xres = sem("s_x_res")
        s_x1 = sem("s_x1")
        s_xn1 = sem("s_xn1")
        s_x1st = sem("s_x1_stored")
        s_xn1st = sem("s_xn1_stored")
        s_gate = sem("s_gate_psum")
        s_dlt = sem("s_gap")
        s_exp = sem("s_exp")
        s_m = sem("s_chosen")
        s_pos = sem("s_pos_psum")
        s_oh = sem("s_onehots")
        s_inf = sem("s_info_mm")
        s_cnt = sem("s_counts_psum")
        s_sel = sem("s_select")
        s_selp = sem("s_slots_psum")
        s_slots = sem("s_slots")

        s_raw = [sem(f"s_raw{i}") for i in range(3)]
        s_ew = sem("s_expert_w")
        s_xg = [sem(f"s_xg{i}") for i in range(YR)]
        s_xs = sem("s_xs")
        s_xep = sem("s_xe_psum")
        s_xehi = sem("s_xe_hi")
        s_xelo = sem("s_xe_lo")
        s_ab = sem("s_up_psum")
        s_sil = sem("s_silu")
        s_he = sem("s_he")
        s_hep = sem("s_heT_psum")
        s_hehi = sem("s_heT_hi")
        s_helo = sem("s_heT_lo")
        s_yp = sem("s_y_psum")
        s_y = sem("s_y")
        s_sc = sem("s_y_added")

        S1 = NC * NT

        block = ctx.enter_context(nc.Block())

        def static(v):
            return isinstance(v, int)

        def expert_load(sp, e, n):
            w = (EW1, EW3, EW2)[n]
            k = (KD, KD, KH)[n]
            one = w[bass.ds(e, 1), :, :].rearrange("o (k p) d -> p (o k) d", k=k)
            sp.dma_start(w_raw[:, n, :].rearrange("p (k d) -> p k d", k=k), one).then_inc(s_raw[n], 16)

        def ew_part(buf, n, lo):
            o = buf * EWS
            if n == 2:
                return ew[:, o + 8 * H + 2 * H * lo:o + 8 * H + 2 * H * (lo + 1)]
            v = ew[:, o + 4 * H * lo:o + 4 * H * (lo + 1)].rearrange("p (k d) -> p k d", k=KD)
            return v[:, :, n * H:(n + 1) * H]

        @block.sync
        def _(sp):
            xv = x.rearrange("(t p) d -> p t d", p=P)
            adj_rows = adj.rearrange("(t p) n -> t p n", p=P)
            for g in range(NC):
                sp.dma_start(x_in[:, CT * g:CT * (g + 1), :], xv[:, CT * g:CT * (g + 1), :]).then_inc(s_x[g], 16)
                if g == 0:
                    for i, w in enumerate((W1, W3, Wf)):
                        sp.dma_start(Wg[:, i, :, :], w.rearrange("(k p) d -> p k d", p=P)).then_inc(s_w, 16)
                    sp.dma_start(bT[:, 0, :], b1.rearrange("(k p) -> p k", p=P),
                                 allow_slow_non_contiguous=True).then_inc(s_w, 16)
                    sp.dma_start(bT[:, 1, :], b3.rearrange("(k p) -> p k", p=P),
                                 allow_slow_non_contiguous=True).then_inc(s_w, 16)
                    sp.dma_start(bf_row[:, :], bf.rearrange("(o d) -> o d", o=1)).then_inc(s_w, 16)
                    sp.dma_start(gw[:, :, :], gate_w.rearrange("(k p) e -> p k e", p=P)).then_inc(s_w, 16)
            for t in range(NT):
                if t >= 2:
                    sp.wait_ge(s_adj[t % 2], 16 * (t // 2))
                if t == NT - 2:
                    sp.wait_ge(s_zp, NT)
                sp.dma_start(adj_s[:, t, :], adj_rows[t, :, :]).then_inc(s_adj[t % 2], 16)
            def residual(c):
                sp.dma_start(x_res[:, :, :], xv[:, CT * c:CT * (c + 1), :]).then_inc(s_xres, 16)

            sp.wait_ge(s_zlo, NT + CT)
            residual(0)
            ov = out[0:N, :].rearrange("(t p) d -> p t d", p=P)
            tv = table[0:N, :].rearrange("(t p) d -> p t d", p=P)
            for c in range(NC):
                sp.wait_ge(s_x1, CT * (c + 1))
                sp.dma_start(ov[:, CT * c:CT * (c + 1), :], x1[:, :, :]).then_inc(s_x1st, 16)
                sp.wait_ge(s_xn1, c + 1)
                sp.dma_start(tv[:, CT * c:CT * (c + 1), :], xn1[:, :, :]).then_inc(s_xn1st, 16)
                if c + 1 < NC:
                    sp.wait_ge(s_xn1st, 16 * (c + 1))
                    sp.wait_ge(s_xtp, NT + CT * (c + 1))
                    residual(c + 1)
                if c == 0:
                    for n in range(3):
                        expert_load(sp, 0, n)
            with sp.Fori(1, E) as e:
                for n in range(3):
                    sp.wait_ge(s_ew, 3 * (e - 1) + n + 1)
                    expert_load(sp, e, n)

        @block.gpsimd
        def _(pool):
            own = [0]

            def settle(ins):
                own[0] += 1
                ins.then_inc(s_pool, 1)
                pool.wait_ge(s_pool, own[0])

            settle(nc.gpsimd.memset(ident[:, :], 0.0))
            nc.gpsimd.affine_select(out=ident[:, :], in_=ident[:, :], compare_op=ALU.not_equal, fill=1.0, base=0,
                                    pattern=[[-1, P]], channel_multiplier=1).then_inc(s_const, 1)
            nc.gpsimd.memset(zero_rows[:, :], 0.0).then_inc(s_const, 1)
            settle(nc.gpsimd.memset(ones_b[:, :], 1.0))
            settle(nc.gpsimd.affine_select(out=tri[:, :], in_=ones_b[:, :], compare_op=ALU.is_gt, fill=0.0, base=0,
                                           pattern=[[1, P]], channel_multiplier=-1))
            nc.gpsimd.memset(one_row[:, :], 1.0)
            nc.gpsimd.iota(iota[:, :], pattern=[[1, P]], base=0, channel_multiplier=0,
                           allow_small_or_imprecise_dtypes=True)
            nc.gpsimd.iota(pcol[:, :], pattern=[[0, 1]], base=0, channel_multiplier=1,
                           allow_small_or_imprecise_dtypes=True)
            nc.gpsimd.iota(vcol[:, :], pattern=[[-P, NT]], base=N, channel_multiplier=-1,
                           allow_small_or_imprecise_dtypes=True)
            settle(nc.gpsimd.memset(m_run[:, :, :], 0.0))
            settle(nc.gpsimd.memset(eq_q[:, :], 1.0))
            settle(nc.gpsimd.affine_select(out=eq_q[:, :], in_=eq_q[:, :], compare_op=ALU.is_ge, fill=0.0, base=0,
                                           pattern=[[-NT, E]], channel_multiplier=1))
            settle(nc.gpsimd.affine_select(out=eq_q[:, :], in_=eq_q[:, :], compare_op=ALU.is_ge, fill=0.0,
                                           base=NT - 1, pattern=[[NT, E]], channel_multiplier=-1)
                   )
            settle(nc.gpsimd.tensor_copy(kq[:, :], pcol[:, :]))
            for e in range(1, E):
                m = nc.gpsimd.tensor_scalar(std[:, 0:1], pcol[:, :], float(NT * e), float(-NT), ALU.is_ge, ALU.mult)
                settle(m)
                settle(nc.gpsimd.tensor_tensor(kq[:, :], kq[:, :], std[:, 0:1], ALU.add))
            nc.gpsimd.memset(std[:, :], 0.0).then_inc(s_const, 1)

            def split(buf, n, loads):
                pool.wait_ge(s_raw[n], loads)
                raw = w_raw[:, n, :]
                if n < 2:
                    raw = raw.rearrange("p (k d) -> p k d", k=KD)
                nc.gpsimd.tensor_scalar(ew_part(buf, n, 0), raw, 1.0, 0.0, ALU.mult, ALU.add).then_inc(s_pool, 1)

            def split_lo(buf, n):
                raw = w_raw[:, n, :]
                if n < 2:
                    raw = raw.rearrange("p (k d) -> p k d", k=KD)
                nc.gpsimd.tensor_tensor(ew_part(buf, n, 1), raw, ew_part(buf, n, 0).bitcast(F32),
                                        ALU.subtract).then_inc(s_ew, 1)

            for e in range(2):
                for n in range(3):
                    if e == 0 and n == 0:
                        pool.wait_ge(s_lo, S1 + 2 * NT)
                    if e == 0 and n == 2:
                        pool.wait_ge(s_lo, S1 + 3 * NT)
                    if e == 1 and n == 0:
                        pool.wait_ge(s_lo, 2 * S1)
                    split(e, n, 16 * (e + 1))
                    own[0] += 1
                    pool.wait_ge(s_pool, own[0])
                    split_lo(e, n)

            pool.wait_ge(s_slots, 1)
            pool.wait_ge(s_zero, 32)
            pool.wait_ge(s_xn1st, 16 * NC)
            pool.wait_ge(s_x1st, 16 * NC)
            for j in range(TILES):
                if j >= YR:
                    pool.wait_ge(s_xg[j % YR], 16 * (j // YR))
                nc.gpsimd.indirect_dma_start(
                    out=xg[:, j, :], out_offset=None, in_=table[:, :],
                    in_offset=bass.IndirectOffsetOnAxis(ap=idx[:, j:j + 1], axis=0),
                    bounds_check=N + P - 1).then_inc(s_xg[j % YR], 16)

            def wait_now(which, value):
                pool.wait_ge(which, value)
                pool.sem_inc(s_alone, 1)

            def tile(j, u):
                if not (static(j) and j == 0):
                    next_expert(j)
                wait_now(s_y, j + 1)
                if not (static(j) and j == 0):
                    wait_now(s_sc, 16 * j)
                nc.gpsimd.indirect_dma_start(
                    out=out[:, :], out_offset=bass.IndirectOffsetOnAxis(ap=idx_st[:, u, :], axis=0),
                    in_=y_st[:, u, :], in_offset=None, bounds_check=N + P - 1,
                    compute_op=ALU.add).then_inc(s_sc, 16)

            def next_expert(j):
                todo = nc.gpsimd.value_load(te_i[0:1, 1, bass.ds(j, 1)], min_val=0, max_val=2)
                load = nc.gpsimd.value_load(te_i[0:1, 0, bass.ds(j, 1)], min_val=0, max_val=E - 1)
                for buf in range(2):
                    with nc.gpsimd.If(todo == buf + 1):
                        wait_now(s_yp, j)
                        for n in range(3):
                            wait_now(s_raw[n], 16 * (load + 2))
                            raw = w_raw[:, n, :]
                            if n < 2:
                                raw = raw.rearrange("p (k d) -> p k d", k=KD)
                            nc.gpsimd.tensor_scalar(ew_part(buf, n, 0), raw, 1.0, 0.0, ALU.mult,
                                                    ALU.add).then_inc(s_pool, 1)
                            wait_now(s_pool, own[0] + 3 * (load - 1) + n + 1)
                            split_lo(buf, n)

            for u in range(YR):
                tile(u, u)
            with nc.gpsimd.Fori(1, TILES // YR) as i:
                for u in range(YR):
                    tile(i * YR + u, u)
            pool.wait_ge(s_sc, 16 * TILES)

        @block.scalar
        def _(act):
            act.wait_ge(s_const, 2)
            act.dma_start(table[N:N + P, :], zero_rows[:, :]).then_inc(s_zero, 16)
            act.dma_start(out[N:N + P, :], zero_rows[:, :]).then_inc(s_zero, 16)

            def roots(n):
                act.wait_ge(s_var, n)
                nc.scalar.activation(std[:, :], mv[:, :, 1], ACT.Sqrt).then_inc(s_sqrt, 1)

            roots(1)
            for t in range(NT + 1):
                if t < NT:
                    act.wait_ge(s_xtp, t + 1)
                    if t >= 2:
                        act.wait_ge(s_zp, t - 1)
                    nc.scalar.copy(xT[:, t % 2, :, :], tp[t % 2][:, 0:D].rearrange("p (k n) -> p k n", k=KD)
                                   ).then_inc(s_xt, 1)
                if t % CT == 1 and t // CT + 1 < NC:
                    roots(t // CT + 2)
                if t >= 1:
                    act.wait_ge(s_zp, t)
                    nc.scalar.copy(Z[:, 0, t - 1, :], sm[(t - 1) % 2][:, 0:D]).then_inc(s_zhi, 1)

            def hi_of_block(s):
                layer, c, jb = s // S1, s % S1 // NT, s % NT
                blk = adj_s[:, CT * c:CT * (c + 1), jb * P:(jb + 1) * P]
                dst = ring[:, s % RING, 0, :].rearrange("p (i n) -> p i n", i=CT)
                if s >= RING:
                    act.wait_ge(s_mm, s - RING + 1)
                if layer == 0:
                    act.wait_ge(s_tp, s + 1)
                    src = tp[s % 2][:, :].rearrange("p (i n) -> p i n", i=CT)
                    nc.scalar.copy(dst, src).then_inc(s_hi, 1)
                    nc.scalar.copy(blk, src).then_inc(s_adjT, 1)
                else:
                    nc.scalar.copy(dst, blk).then_inc(s_hi, 1)

            def hidden(layer, c):
                n = layer * NC + c
                act.wait_ge(s_mm, NT * (n + 1))
                if layer == 0 and c == 0:
                    act.wait_ge(s_zero, 32)
                if n >= 2:
                    if n - 2 < NC:
                        act.wait_ge(s_z2p, CT * (n - 1))
                    else:
                        act.wait_ge(s_up, CT * (n - 1 - NC))
                for f in range(KD):
                    last = nc.scalar.activation(hT[:, n % 2, f, :], acc[n % 2][f][:, :], ACT.Relu,
                                                bias=bT[:, layer, f:f + 1])
                last.then_inc(s_h, 1)

            def z_hi(t):
                act.wait_ge(s_z2, t + 1)
                act.wait_ge(s_mm, S1 - NT + t + 1)
                nc.scalar.copy(Z[:, 0, t, :], z2[:, t, :]).then_inc(s_zhi, 1)

            def token_work(c, k):
                if k in (3, 4):
                    for i in (2 * k - 6, 2 * k - 5):
                        t = CT * c + i
                        act.wait_ge(s_up, t + 1)
                        if c >= 1:
                            act.wait_ge(s_x1st, 16 * c)
                        nc.scalar.activation(x1[:, i, :], sm[i % 2][:, 0:D], ACT.Tanh).then_inc(s_th, 1)
                if k == 5:
                    roots(NC + c + 1)
                if k in (8, 9):
                    for i in (2 * k - 16, 2 * k - 15):
                        t = NT + CT * c + i
                        act.wait_ge(s_xtp, t + 1)
                        if i >= 2:
                            act.wait_ge(s_gate, CT * c + i - 1)
                        nc.scalar.copy(xT[:, i % 2, :, :],
                                       xn_p[i % 2][:, 0:D].rearrange("p (k n) -> p k n", k=KD)).then_inc(s_xt, 1)
                if k == 11:
                    act.wait_ge(s_dlt, c + 1)
                    nc.scalar.activation(ex[:, :], dlt[:, :], ACT.Exp).then_inc(s_exp, 1)

            for s in range(2 * S1):
                layer, c, jb = s // S1, s % S1 // NT, s % NT
                if s == S1:
                    act.wait_ge(s_adjT, S1)
                hi_of_block(s)
                if jb == 1 and s > NT:
                    n = s // NT - 1
                    hidden(n // NC, n % NC)
                if layer == 0 and c == NC - 1 and 2 <= jb < NT - CT + 2:
                    z_hi(jb - 2)
                if layer == 1 and c == 0 and 5 <= jb < 5 + CT:
                    z_hi(NT - CT + jb - 5)
                if layer == 1 and c >= 1:
                    token_work(c - 1, jb)
            hidden(1, NC - 1)
            for k in range(NT):
                token_work(NC - 1, k)

            def xe_hi(j):
                act.wait_ge(s_xep, j + 1)
                if not (static(j) and j == 0):
                    act.wait_ge(s_ab, 2 * j)
                nc.scalar.copy(xeT[:, 0, :, :], xe_p[:, 0:D].rearrange("p (k n) -> p k n", k=KD)).then_inc(s_xehi, 1)

            def y_out(j, u):
                act.wait_ge(s_yp, j + 1)
                if not static(j) or j >= YR:
                    act.wait_ge(s_sc, 16 * (j - YR + 1))
                nc.scalar.copy(idx_st[:, u, :], idx[:, bass.ds(j, 1)])
                nc.scalar.activation(y_st[:, u, :], y_p[:, 0:D], ACT.Copy,
                                     scale=wt[:, bass.ds(j, 1)]).then_inc(s_y, 1)

            def tile(j, u):
                for h in range(2):
                    act.wait_ge(s_ab, 2 * j + h + 1)
                    if not (static(j) and j == 0):
                        act.wait_ge(s_he, 2 * j + h - 1)
                    nc.scalar.activation(sil[:, h, :], up_p[h][:, :], ACT.Silu).then_inc(s_sil, 1)
                if not (static(j) and j == TILES - 1):
                    xe_hi(j + 1)
                if not (static(j) and j == 0):
                    y_out(j - 1, (u - 1) % YR)
                for h in range(2):
                    act.wait_ge(s_hep, 2 * j + h + 1)
                    nc.scalar.copy(heT[:, 0, CT * h:CT * (h + 1), :],
                                   heT_p[h][:, :].rearrange("p (k n) -> p k n", k=CT)).then_inc(s_hehi, 1)

            xe_hi(0)
            for u in range(YR):
                tile(u, u)
            with act.Fori(1, TILES // YR - 1) as i:
                for u in range(YR):
                    tile(i * YR + u, u)
            for u in range(YR):
                tile(TILES - YR + u, u)
            y_out(TILES - 1, YR - 1)

        @block.vector
        def _(dve):
            own = [0]

            def settle(ins):
                own[0] += 1
                ins.then_inc(s_dve, 1)
                dve.wait_ge(s_dve, own[0])

            def norm(src, n, done):
                for i in range(CT):
                    st = nc.vector.bn_stats(stats[:, i, :], src(i))
                settle(st)
                for i in range(CT):
                    st = nc.vector.bn_aggr(mv[:, i, :], stats[:, i, :])
                settle(st)
                nc.vector.tensor_scalar(mv[:, :, 1], mv[:, :, 1], EPS, None, ALU.add).then_inc(s_var, 1)
                dve.wait_ge(s_sqrt, n)
                settle(nc.vector.reciprocal(rstd[:, :], std[:, :]))

            dve.wait_ge(s_const, 3)
            for g in range(NC + 1):
                if g < NC:
                    dve.wait_ge(s_x[g], 16)
                    norm(lambda i: x_in[:, CT * g + i, :], g + 1, None)
                    for i in range(CT):
                        v = x_in[:, CT * g + i, :]
                        last = nc.vector.tensor_scalar(v, v, mv[:, i, 0:1], rstd[:, i:i + 1], ALU.subtract, ALU.mult)
                    last.then_inc(s_xn, 1)
                if g >= 1:
                    for t in range(CT * (g - 1), CT * g):
                        dve.wait_ge(s_zhi, t + 1)
                        nc.vector.tensor_tensor(Z[:, 1, t, :], sm[t % 2][:, 0:D], Z[:, 0, t, :].bitcast(F32),
                                                ALU.subtract).then_inc(s_zlo, 1)

            def lo_of_block(s):
                layer, c, jb = s // S1, s % S1 // NT, s % NT
                if layer == 0:
                    dve.wait_ge(s_adjT, s + 1)
                else:
                    dve.wait_ge(s_hi, s + 1)
                hi = ring[:, s % RING, 0, :].bitcast(F32).rearrange("p (i n) -> p i n", i=CT)
                lo = ring[:, s % RING, 1, :].rearrange("p (i n) -> p i n", i=CT)
                src = adj_s[:, CT * c:CT * (c + 1), jb * P:(jb + 1) * P]
                nc.vector.tensor_tensor(lo, src, hi, ALU.subtract).then_inc(s_lo, 1)

            def z_lo(t):
                dve.wait_ge(s_zhi, NT + t + 1)
                nc.vector.tensor_tensor(Z[:, 1, t, :], z2[:, t, :], Z[:, 0, t, :].bitcast(F32),
                                        ALU.subtract).then_inc(s_zlo, 1)

            def z2_out(t):
                dve.wait_ge(s_z2p, t + 1)
                nc.vector.tensor_copy(z2[:, t, :], sm[t % 2][:, 0:D]).then_inc(s_z2, 1)

            def bc(v, n):
                return v.unsqueeze(len(v.shape)).to_broadcast(list(v.shape) + [n])

            def token_work(c, k):
                if k in (3, 4):
                    for i in (2 * k - 6, 2 * k - 5):
                        t = CT * c + i
                        dve.wait_ge(s_th, t + 1)
                        dve.wait_ge(s_xres, 16 * (c + 1))
                        nc.vector.tensor_tensor(x1[:, i, :], x1[:, i, :], x_res[:, i, :], ALU.add).then_inc(s_x1, 1)
                if k == 5:
                    dve.wait_ge(s_x1, CT * (c + 1))
                    norm(lambda i: x1[:, i, :], NC + c + 1, None)
                    for i in range(CT):
                        last = nc.vector.tensor_scalar(xn1[:, i, :], x1[:, i, :], mv[:, i, 0:1], rstd[:, i:i + 1],
                                                       ALU.subtract, ALU.mult)
                    last.then_inc(s_xn1, 1)
                if k == 10:
                    dve.wait_ge(s_gate, CT * (c + 1))
                    g = gate_p.rearrange("p (i e) -> p i e", e=E)
                    for i in range(CT):
                        last = nc.vector.max(out=m8[:, i, :], in_=g[:, i, :])
                    settle(last)
                    for i in range(CT):
                        last = nc.vector.max_index(out=ix8[:, i, :], in_max=m8[:, i, :], in_values=g[:, i, :])
                    settle(last)
                    nc.vector.tensor_tensor(dlt[:, :], m8[:, :, 1], m8[:, :, 0], ALU.subtract).then_inc(s_dlt, 1)
                    settle(nc.vector.tensor_copy(idxf[:, :, :], ix8[:, :, 0:2].rearrange("p i k -> p k i")))
                    io = iota[:, 0:E].unsqueeze(1).to_broadcast([P, 2 * CT, E])
                    ohv = oh[:, :, :, :].rearrange("p k i e -> p (k i) e")
                    settle(nc.vector.tensor_tensor(ohv, io, bc(idxf.rearrange("p k i -> p (k i)"), E), ALU.is_equal))
                    if c >= 1:
                        settle(nc.vector.tensor_copy(m_run[:, 0, :], m_run[:, CT, :]))
                    mb = m_bf[:, 0, :].rearrange("p (i e) -> p i e", e=E)
                    settle(nc.vector.tensor_tensor(mb, oh[:, 0, :, :], oh[:, 1, :, :], ALU.add))
                    for i in range(CT):
                        settle(nc.vector.tensor_tensor(m_run[:, i + 1, :], m_run[:, i, :], mb[:, i, :], ALU.add))
                    nc.vector.tensor_copy(m_bf[:, 1, :].rearrange("p (i e) -> p i e", e=E),
                                          m_run[:, 0:CT, :]).then_inc(s_m, 1)
                if k == 12:
                    dve.wait_ge(s_exp, c + 1)
                    settle(nc.vector.tensor_scalar(wk[:, 1, :], ex[:, :], 1.0, None, ALU.add))
                    settle(nc.vector.reciprocal(wk[:, 0, :], wk[:, 1, :]))
                    settle(nc.vector.tensor_tensor(wk[:, 1, :], ex[:, :], wk[:, 0, :], ALU.mult))
                    wkf = wk.rearrange("p k i -> p (k i)")
                    settle(nc.vector.tensor_copy(whi[:, 0, :], wkf))
                    settle(nc.vector.tensor_tensor(whi[:, 1, :], wkf, whi[:, 0, :].bitcast(F32), ALU.subtract))
                    dve.wait_ge(s_pos, c + 1)
                    for k2 in range(2):
                        last = nc.vector.tensor_tensor(ohpos[:, k2, :, :], oh[:, k2, :, :],
                                                       pos_p.rearrange("p (i e) -> p i e", e=E), ALU.mult)
                    settle(last)
                    settle(nc.vector.tensor_reduce(posk[:, :, :], ohpos[:, :, :, :], AX.X, ALU.add))
                    settle(nc.vector.scalar_tensor_tensor(
                        out=gsl[:, :], in0=idxf.rearrange("p k i -> p (k i)"), scalar=float(N),
                        in1=posk.rearrange("p k i -> p (k i)"), op0=ALU.mult, op1=ALU.add))
                    shift = P.bit_length() - 1
                    nc.vector.tensor_scalar(qi[:, :], gsl[:, :], shift, None, ALU.logical_shift_right)
                    settle(nc.vector.tensor_scalar(si[:, :], gsl[:, :], P - 1, None, ALU.bitwise_and))
                    nc.vector.tensor_copy(qf[:, :], qi[:, :])
                    settle(nc.vector.tensor_copy(sf[:, :], si[:, :]))
                if k in (13, 14):
                    for n in range(4 * (k - 13), 4 * (k - 13) + 4):
                        m = 2 * CT * c + n
                        t = CT * c + n % CT
                        if m >= 2:
                            dve.wait_ge(s_inf, m - 1)
                        nc.vector.tensor_scalar(oh_q[:, m % 2, :], iota[:, :], qf[:, n:n + 1], None, ALU.is_equal)
                        vals = (vcol[:, t:t + 1], whi[:, 0, n:n + 1].bitcast(F32), whi[:, 1, n:n + 1].bitcast(F32))
                        for r, v in enumerate(vals):
                            last = nc.vector.tensor_scalar(oh_s[:, m % 2, r * P:(r + 1) * P], iota[:, :],
                                                           sf[:, n:n + 1], v, ALU.is_equal, ALU.mult)
                        last.then_inc(s_oh, 1)

            for s in range(2 * S1):
                layer, c, jb = s // S1, s % S1 // NT, s % NT
                if s == S1:
                    dve.wait_ge(s_adjT, S1)
                lo_of_block(s)
                if layer == 0 and c >= 1 and jb in (3, 4):
                    z2_out(CT * (c - 1) + 2 * jb - 6)
                    z2_out(CT * (c - 1) + 2 * jb - 5)
                if layer == 1 and c == 0 and jb in (3, 4):
                    z2_out(NT - CT + 2 * jb - 6)
                    z2_out(NT - CT + 2 * jb - 5)
                if layer == 0 and c == NC - 1 and 2 <= jb < NT - CT + 2:
                    z_lo(jb - 2)
                if layer == 1 and c == 0 and 5 <= jb < 5 + CT:
                    z_lo(NT - CT + jb - 5)
                if layer == 1 and c >= 1:
                    token_work(c - 1, jb)
            for k in range(NT):
                token_work(NC - 1, k)

            mb = m_bf[:, 0, 0:E]
            dve.wait_ge(s_pos, NC)
            nc.vector.tensor_copy(mb, m_run[:, CT, :]).then_inc(s_m, 1)
            dve.wait_ge(s_cnt, 1)
            settle(nc.vector.tensor_scalar(cnt_i[:, :], cnt_p, float(P - 1), None, ALU.add))
            settle(nc.vector.tensor_scalar(cnt_i[:, :], cnt_i[:, :], P.bit_length() - 1, None,
                                           ALU.logical_shift_right))
            settle(nc.vector.tensor_copy(cnt[:, :], cnt_i[:, :]))
            settle(nc.vector.tensor_scalar(tl[:, 1, :], cnt[:, :], 1.0, None, ALU.max))
            settle(nc.vector.memset(cnt[:, :], 1.0))
            settle(nc.vector.tensor_tensor_scan(end[:, :], cnt[:, :], tl[:, 1, :], 0.0, ALU.mult, ALU.add))
            settle(nc.vector.tensor_tensor(tl[:, 0, :], end[:, :], tl[:, 1, :], ALU.subtract))
            tq = tmp_j[:, 0:2 * E].rearrange("p (a e) -> p a e", a=2)
            for a in range(2):
                last = nc.vector.tensor_tensor(tq[:, a, :], tl[:, a, :], eq_q[:, :], ALU.mult)
            settle(last)
            settle(nc.vector.tensor_reduce(sq[:, :], tq, AX.X, ALU.add))
            settle(nc.vector.tensor_scalar(sq[:, 0:1], sq[:, 0:1], kq[:, :], 1.0, ALU.add, ALU.add))
            settle(nc.vector.tensor_tensor(sq[:, 1:2], kq[:, :], sq[:, 1:2], ALU.is_lt))
            settle(nc.vector.tensor_scalar(sq[:, 0:1], sq[:, 0:1], sq[:, 1:2], -1.0, ALU.mult, ALU.add))
            settle(nc.vector.tensor_scalar(sel[:, 0:TILES], iota[:, 0:TILES], sq[:, 0:1], None, ALU.is_equal))
            dve.wait_ge(s_inf, 2 * NT)
            nc.vector.tensor_copy(info[:, 0, :], info_p[:, 0:P])
            settle(nc.vector.tensor_copy(info[:, 1, :], info_p[:, P:2 * P]))
            nc.vector.tensor_tensor(info[:, 1, :], info[:, 1, :], info_p[:, 2 * P:3 * P], ALU.add).then_inc(s_sel, 1)
            cmp = tmp_j[0:1, 16:16 + TILES * (E - 1)].rearrange("p (j e) -> p j e", e=E - 1)
            te = tmp_j[0:1, 400:400 + 3 * TILES].rearrange("p (a j) -> p a j", a=3)
            ej = end[0:1, 0:E - 1].unsqueeze(1).to_broadcast([1, TILES, E - 1])
            settle(nc.vector.tensor_tensor(cmp, ej, bc(iota[0:1, 0:TILES], E - 1), ALU.is_le))
            settle(nc.vector.tensor_reduce(te[:, 0, :], cmp, AX.X, ALU.add))
            settle(nc.vector.tensor_copy(te_i[:, 0, :], te[:, 0, :]))
            settle(nc.vector.tensor_scalar(te[:, 1, :], te[:, 0, :], 1.0, None, ALU.add))
            settle(nc.vector.tensor_copy(te_i[:, 1, :], te[:, 1, :]))
            settle(nc.vector.tensor_scalar(te_i[:, 1, :], te_i[:, 1, :], 1, None, ALU.bitwise_and))
            settle(nc.vector.tensor_copy(te[:, 1, :], te_i[:, 1, :]))
            settle(nc.vector.tensor_scalar(te[:, 1, :], te[:, 1, :], 1.0, None, ALU.add))
            settle(nc.vector.memset(te[:, 2, 0:1], 0.0))
            settle(nc.vector.tensor_tensor(te[:, 2, 1:TILES], te[:, 0, 1:TILES], te[:, 0, 0:TILES - 1], ALU.subtract))
            settle(nc.vector.tensor_tensor(te[:, 1, :], te[:, 1, :], te[:, 2, :], ALU.mult))
            settle(nc.vector.tensor_scalar(te[:, 2, :], te[:, 0, :], float(E - 2), None, ALU.is_le))
            settle(nc.vector.tensor_tensor(te_i[:, 1, :], te[:, 1, :], te[:, 2, :], ALU.mult))
            dve.wait_ge(s_selp, 1)
            pad = tmp_j[:, 640:640 + TILES]
            settle(nc.vector.tensor_scalar(pad, sel_p[:, 0, :], 0.0, pcol[:, :], ALU.is_equal, ALU.mult))
            settle(nc.vector.tensor_tensor(pad, pad, sel_p[:, 0, :], ALU.subtract))
            nc.vector.tensor_scalar(idx[:, :], pad, float(N), None, ALU.add)
            nc.vector.tensor_copy(wt[:, :], sel_p[:, 1, :]).then_inc(s_slots, 1)

            def row_copy(j, u, i):
                dve.wait_ge(s_xg[u], 16 * (i + 1))
                if not (static(j) and j == 0):
                    dve.wait_ge(s_xep, j)
                nc.vector.tensor_copy(xs[:, :], xg[:, bass.ds(j, 1), :].rearrange("p o d -> p (o d)")).then_inc(s_xs, 1)

            def xe_lo(j):
                dve.wait_ge(s_xehi, j + 1)
                nc.vector.tensor_tensor(xeT[:, 1, :, :], xe_p[:, 0:D].rearrange("p (k n) -> p k n", k=KD),
                                        xeT[:, 0, :, :].bitcast(F32), ALU.subtract).then_inc(s_xelo, 1)

            def tile(j, u, i):
                if not (static(j) and j == TILES - 1):
                    row_copy(j + 1, (u + 1) % YR, i + (u + 1) // YR)
                for h in range(2):
                    dve.wait_ge(s_sil, 2 * j + h + 1)
                    if not (static(j) and j == 0):
                        dve.wait_ge(s_hep, 2 * j)
                    nc.vector.tensor_tensor(he[:, h * HW:(h + 1) * HW], sil[:, h, :], up_p[2 + h][:, :],
                                            ALU.mult).then_inc(s_he, 1)
                if not (static(j) and j == TILES - 1):
                    xe_lo(j + 1)
                for h in range(2):
                    dve.wait_ge(s_hehi, 2 * j + h + 1)
                    nc.vector.tensor_tensor(heT[:, 1, CT * h:CT * (h + 1), :],
                                            heT_p[h][:, :].rearrange("p (k n) -> p k n", k=CT),
                                            heT[:, 0, CT * h:CT * (h + 1), :].bitcast(F32),
                                            ALU.subtract).then_inc(s_helo, 1)

            row_copy(0, 0, 0)
            xe_lo(0)
            for u in range(YR):
                tile(u, u, 0)
            with dve.Fori(1, TILES // YR - 1) as i:
                for u in range(YR):
                    tile(i * YR + u, u, i)
            for u in range(YR):
                tile(TILES - YR + u, u, TILES // YR - 1)

        @block.tensor
        def _(pe):
            pe.wait_ge(s_const, 3)
            pe.wait_ge(s_w, 7 * 16)

            for t in range(NT + 1):
                if t < NT:
                    pe.wait_ge(s_xn, t // CT + 1)
                    if t >= 2:
                        pe.wait_ge(s_xt, t - 1)
                    for k in range(KD):
                        last = nc.tensor.transpose(tp[t % 2][:, k * P:(k + 1) * P], x_in[:, t, k * P:(k + 1) * P],
                                                   ident[:, :])
                    last.then_inc(s_xtp, 1)
                if t >= 1:
                    m = t - 1
                    pe.wait_ge(s_xt, t)
                    if m >= 2:
                        pe.wait_ge(s_zlo, m - 1)
                    for k in range(KD):
                        last = nc.tensor.matmul(sm[m % 2][:, 0:D], xT[:, m % 2, k, :], Wg[:, 0, k, :],
                                                start=(k == 0), stop=(k == KD - 1))
                    last.then_inc(s_zp, 1)

            def transpose_block(s):
                c, jb = s // NT, s % NT
                if jb == 0:
                    for par in range(2):
                        pe.wait_ge(s_adj[par], 16 * (CT * (c + 1) // 2))
                if s >= 2:
                    pe.wait_ge(s_adjT, s - 1)
                else:
                    pe.wait_ge(s_xt, NT)
                for i in range(CT):
                    last = nc.tensor.transpose(tp[s % 2][:, i * P:(i + 1) * P],
                                               adj_s[:, CT * c + i, jb * P:(jb + 1) * P], ident[:, :])
                last.then_inc(s_tp, 1)

            def product(s):
                n, jb = s // NT, s % NT
                pe.wait_ge(s_lo, s + 1)
                if n == 0:
                    pe.wait_ge(s_zlo, jb + 1)
                if n == NC:
                    pe.wait_ge(s_zlo, NT + jb + 1)
                if jb == 0 and n >= 2:
                    pe.wait_ge(s_h, n - 1)
                hi, lo = ring[:, s % RING, 0, :], ring[:, s % RING, 1, :]
                for f in range(KD):
                    zh = Z[:, 0, jb, f * P:(f + 1) * P]
                    zl = Z[:, 1, jb, f * P:(f + 1) * P]
                    a = acc[n % 2][f][:, :]
                    nc.tensor.matmul(a, zh, hi, start=(jb == 0), stop=False)
                    nc.tensor.matmul(a, zh, lo, start=False, stop=False)
                    last = nc.tensor.matmul(a, zl, hi, start=False, stop=(jb == NT - 1))
                last.then_inc(s_mm, 1)

            def z2_rows(t):
                c = t // CT
                pe.wait_ge(s_h, c + 1)
                if t >= 2:
                    pe.wait_ge(s_z2, t - 1)
                for k in range(KD):
                    last = nc.tensor.matmul(sm[t % 2][:, 0:D], hT[:, c % 2, k, (t % CT) * P:(t % CT + 1) * P],
                                            Wg[:, 1, k, :], start=(k == 0), stop=(k == KD - 1))
                last.then_inc(s_z2p, 1)

            def token_work(c, k):
                if k in (2, 3):
                    for i in (2 * k - 4, 2 * k - 3):
                        t = CT * c + i
                        pe.wait_ge(s_h, NC + c + 1)
                        if i >= 2:
                            pe.wait_ge(s_th, t - 1)
                        elif c == 0:
                            pe.wait_ge(s_z2, NT)
                        else:
                            pe.wait_ge(s_oh, 2 * CT * c)
                        nc.tensor.matmul(sm[i % 2][:, 0:D], one_row[:, :], bf_row[:, :], start=True, stop=False)
                        for f in range(KD):
                            last = nc.tensor.matmul(sm[i % 2][:, 0:D], hT[:, c % 2, f, i * P:(i + 1) * P],
                                                    Wg[:, 2, f, :], start=False, stop=(f == KD - 1))
                        last.then_inc(s_up, 1)
                if k in (7, 8):
                    for i in (2 * k - 14, 2 * k - 13):
                        pe.wait_ge(s_xn1, c + 1)
                        if i >= 2:
                            pe.wait_ge(s_xt, NT + CT * c + i - 1)
                        for f in range(KD):
                            last = nc.tensor.transpose(xn_p[i % 2][:, f * P:(f + 1) * P],
                                                       xn1[:, i, f * P:(f + 1) * P], ident[:, :])
                        last.then_inc(s_xtp, 1)
                        if i < 2:
                            continue
                        gate(c, i - 2)
                if k == 9:
                    gate(c, 2)
                    gate(c, 3)
                if k == 11:
                    pe.wait_ge(s_m, c + 1)
                    nc.tensor.matmul(pos_p, tri[:, :], m_bf[:, 0, :], start=True, stop=False)
                    nc.tensor.matmul(pos_p, ones_b[:, :], m_bf[:, 1, :], start=False, stop=True).then_inc(s_pos, 1)
                if k in (13, 14):
                    for n in range(4 * (k - 13), 4 * (k - 13) + 4):
                        m = 2 * CT * c + n
                        pe.wait_ge(s_oh, m + 1)
                        nc.tensor.matmul(info_p[:, 0:3 * P], oh_q[:, m % 2, :], oh_s[:, m % 2, :], start=(m == 0),
                                         stop=(m == 2 * NT - 1)).then_inc(s_inf, 1)

            def gate(c, i):
                pe.wait_ge(s_xt, NT + CT * c + i + 1)
                for f in range(KD):
                    last = nc.tensor.matmul(gate_p[:, i * E:(i + 1) * E], xT[:, i % 2, f, :], gw[:, f, :],
                                            start=(f == 0), stop=(f == KD - 1))
                last.then_inc(s_gate, 1)

            transpose_block(0)
            for s in range(2 * S1):
                layer, c, jb = s // S1, s % S1 // NT, s % NT
                if s + 1 < S1:
                    transpose_block(s + 1)
                product(s)
                if NT <= s < S1 + NT and jb in (2, 3):
                    z2_rows(CT * (s // NT - 1) + 2 * jb - 4)
                    z2_rows(CT * (s // NT - 1) + 2 * jb - 3)
                if layer == 1 and c >= 1:
                    token_work(c - 1, jb)
            for k in range(NT):
                token_work(NC - 1, k)
            pe.wait_ge(s_m, NC + 1)
            nc.tensor.matmul(cnt_p, ones_b[:, :], m_bf[:, 0, 0:E], start=True, stop=True).then_inc(s_cnt, 1)
            pe.wait_ge(s_sel, 1)
            for a in range(2):
                last = nc.tensor.matmul(sel_p[:, a, :], info[:, a, :], sel[:, 0:TILES], start=True, stop=True)
            last.then_inc(s_selp, 1)

            def rows_T(j):
                pe.wait_ge(s_xs, j + 1)
                if not (static(j) and j == 0):
                    pe.wait_ge(s_xelo, j)
                for k in range(KD):
                    last = nc.tensor.transpose(xe_p[:, k * P:(k + 1) * P], xs[:, k * P:(k + 1) * P], ident[:, :])
                last.then_inc(s_xep, 1)

            def expert_of(j):
                return nc.tensor.value_load(te_i[0:1, 0, bass.ds(j, 1)], min_val=0, max_val=E - 1)

            def three(out_ap, k0, k1, stat, w_at, n):
                for k in range(k0, k1):
                    for sl, wl in ((0, 0), (0, 1), (1, 0)):
                        last = nc.tensor.matmul(out_ap, stat[:, sl, k, :], w_at(k, wl),
                                                start=(k == k0 and sl == wl == 0), stop=(k == k1 - 1 and sl == 1))
                return last

            def up(j):
                e = expert_of(j)
                off = (e % 2) * EWS
                pe.wait_ge(s_ew, 3 * e + 2)
                pe.wait_ge(s_xelo, j + 1)
                for h in range(2):
                    if not (static(j) and j == 0):
                        pe.wait_ge(s_he, 2 * j - 1 + h)
                    for m in range(2):
                        o = m * H + h * HW
                        last = three(up_p[2 * m + h][:, :], 0, KD, xeT,
                                     lambda k, lo: ew[:, bass.ds(off + 4 * H * lo + 2 * H * k + o, HW)], HW)
                    last.then_inc(s_ab, 1)

            def down(j):
                e = expert_of(j)
                off = (e % 2) * EWS
                pe.wait_ge(s_ew, 3 * e + 3)
                pe.wait_ge(s_helo, 2 * j + 2)
                if not (static(j) and j == 0):
                    pe.wait_ge(s_y, j)
                three(y_p[:, 0:D], 0, KH, heT,
                      lambda k, lo: ew[:, bass.ds(off + 8 * H + 2 * H * lo + D * k, D)], D).then_inc(s_yp, 1)

            def hidden_T(j):
                for h in range(2):
                    pe.wait_ge(s_he, 2 * j + h + 1)
                    for k in range(CT):
                        last = nc.tensor.transpose(heT_p[h][:, k * P:(k + 1) * P],
                                                   he[:, (CT * h + k) * P:(CT * h + k + 1) * P], ident[:, :])
                    last.then_inc(s_hep, 1)

            def tile(j):
                up(j)
                if not (static(j) and j == TILES - 1):
                    rows_T(j + 1)
                if not (static(j) and j == 0):
                    down(j - 1)
                hidden_T(j)

            rows_T(0)
            tile(0)
            with pe.Fori(1, TILES - 1) as j:
                tile(j)
            tile(TILES - 1)
            down(TILES - 1)


_INS = ['x', 'adj', 'L0_gnn_W1', 'L0_gnn_b1', 'L0_gnn_W3', 'L0_gnn_b3', 'L0_gnn_Wf', 'L0_gnn_bf', 'L0_ffn_gate_w',
        'L0_ffn_W1', 'L0_ffn_W2', 'L0_ffn_W3']


def kernel(**inputs):
    import numpy as np
    import concourse.bacc as bacc
    from concourse.bass_utils import run_bass_kernel_spmd

    nc = bacc.Bacc("TRN2", target_bir_lowering=False, num_devices=1)
    arrays, args = {}, []
    for name in _INS:
        a = np.ascontiguousarray(inputs[name])
        arrays[f"in_{name}"] = a
        args.append(nc.dram_tensor(f"in_{name}", a.shape, mybir.dt.from_np(a.dtype), kind="ExternalInput").ap())
    n, d = inputs['x'].shape
    o = nc.dram_tensor("out_0", (n + nc.NUM_PARTITIONS, d), F32, kind="ExternalOutput").ap()
    gnn_and_routed_ffn(nc, *args, o)
    r = run_bass_kernel_spmd(nc, [arrays], core_ids=[0])
    return r.results[0]["out_0"][:n]
```

```python
import concourse.bass as bass
from concourse import mybir
from concourse.alu_op_type import AluOpType as ALU
from contextlib import ExitStack

F32 = mybir.dt.float32
F32R = mybir.dt.float32r
BF16 = mybir.dt.bfloat16
I32 = mybir.dt.int32
U32 = mybir.dt.uint32
ACT = mybir.ActivationFunctionType
AX = mybir.AxisListType


def gnn_and_routed_ffn(nc, x, adj, W1, b1, W3, b3, Wf, bf, gate_w, EW1, EW2, EW3, out):
    P = nc.NUM_PARTITIONS
    N, D = x.shape
    E, _, H = EW1.shape
    KD = D // P
    KH = H // P
    NT = N // P
    CT = 4
    NC = NT // CT
    CW = CT * P
    TOPK = 2
    TILES = (TOPK * N + E * (P - 1)) // P
    EPS = 1e-5
    HW = 512
    RING = 3
    YR = 3
    assert TILES % YR == 0 and NT * E == P and KD == 2

    table = nc.dram_tensor("ffn_in_rows", (N + P, D), F32).ap()

    ctx = ExitStack()
    with ctx:
        def sem(name):
            return ctx.enter_context(nc.semaphore(name))

        KB = 1024
        arena = ctx.enter_context(nc.sbuf_tensor("arena", [P, 202 * KB // 4], F32))
        base = 16512

        def at(name, shape, dtype, kb):
            return nc.alloc_sbuf_tensor_at(name, shape, dtype, offset=base + int(kb * KB))

        adj_s = at("adj_s", [P, NT, N], F32, 0)
        x_in = at("x_in", [P, NT, D], F32, 112)
        Z = at("Z", [P, 2, NT, D], F32R, 128)
        z2 = at("z2", [P, NT, D], F32, 160)
        x_res = at("x_res", [P, CT, D], F32, 160)
        x1 = at("x1", [P, CT, D], F32, 164)
        xn1 = x_res
        xT = at("xT", [P, CT, KD, P], F32, 168)
        oh_q = at("oh_q", [P, 2, P], F32R, 172)
        oh_s = at("oh_s", [P, 2, 3 * P], F32R, 173)
        zero_rows = at("zero_rows", [P, D], F32, 176)
        bf_in = at("bf_in", [2, D], F32, 177)
        bf_hi = at("bf_hi", [2, D], F32R, 178)
        hT = at("hT", [P, 2, KD, CW], F32, 176)
        ring = at("ring", [P, RING, 2, CW], F32R, 184)
        Wg = at("Wg", [P, 3, KD, D], F32, 196)
        oh_m = at("oh_m", [P, 2, P], F32, 198)
        route = at("route", [P, KB // 2], F32, 196)
        w_raw = at("w_raw", [P, 3, 2 * H], F32, 0)
        EWS = 12 * H
        ew = at("ew", [P, 2 * EWS], F32R, 24)
        xg = at("xg", [P, TILES, D], F32, 120)
        heT = at("heT", [P, 2, KH, P], F32R, 160)
        he = at("he", [P, H], F32, 168)
        sil = at("sil", [P, 2, HW], F32, 172)
        y_st = at("y_st", [P, YR, D], F32, 176)
        xs = at("xs", [P, D], F32, 179)
        xeT = at("xeT", [P, 2, KD, P], F32R, 184)

        def sb(name, shape, dt):
            return ctx.enter_context(nc.sbuf_tensor(name, shape, dt))

        ident = sb("ident", [P, P], F32)
        iota = sb("iota", [P, P], F32)
        tri = sb("tri", [P, P], BF16)
        ones_b = sb("ones_b", [P, P], BF16)
        bf_parts = sb("bf_parts", [2, D], F32R)
        one_rows = sb("one_rows", [2, P], F32R)
        gw = sb("gw", [P, KD, E], F32)
        bT = sb("bT", [P, 2, KD], F32)
        m_run = sb("m_run", [P, CT + 1, E], F32)
        pcol = sb("pcol", [P, 1], F32)
        idx = sb("idx", [P, TILES], I32)
        wt = sb("wt", [P, TILES], F32)
        idx_st = sb("idx_st", [P, YR, 1], I32)

        used = [0]

        def cut(*shape):
            n = 1
            for s in shape:
                n *= s
            v = route[:, used[0]:used[0] + n]
            used[0] += n
            if len(shape) == 1:
                return v
            names = " ".join("abcd"[:len(shape)])
            return v.rearrange(f"p ({names}) -> p {names}", **dict(zip("abcd", shape)))

        stats = sb("stats", [P, CT, 6], F32)
        mv = sb("mv", [P, CT, 2], F32)
        std = sb("std", [P, CT], F32)
        rstd = sb("rstd", [P, CT], F32)
        m8 = cut(CT, E)
        ix8 = cut(CT, E).bitcast(U32)
        oh = cut(2, CT, E)
        ohpos = cut(2, CT, E)
        idxf = cut(2, CT)
        dlt = cut(CT)
        ex = cut(CT)
        wk = cut(2, CT)
        gsl = cut(2 * CT).bitcast(I32)
        qi = cut(2 * CT).bitcast(I32)
        si = cut(2 * CT).bitcast(I32)
        qf = cut(2 * CT)
        sf = cut(2 * CT)
        posk = cut(2, CT)
        cnt = cut(E)
        cnt_i = cut(E).bitcast(I32)
        tl = cut(2, E)
        end = cut(E)
        sq = cut(2)
        vcol = sb("vcol", [P, NT], F32)
        eq_q = sb("eq_q", [P, E], F32)
        kq = sb("kq", [P, 1], F32)
        bf_sign = sb("bf_sign", [2, 1], F32)
        m_bf = sb("m_bf", [P, 3, CT * E], BF16)
        whi = sb("whi", [P, 2, 2 * CT], F32R)
        info = at("info", [P, 2, P], F32, 184)
        sel = at("sel", [P, P], F32, 185)
        tmp_j = at("tmp_j", [P, 8 * P], F32, 186)
        te_i = sb("te_i", [1, TILES + 2], I32)
        te_f = sb("te_f", [1, 4, TILES + 1], F32)

        bank = [ctx.enter_context(nc.psum_tensor(f"bank{i}", [P, HW], F32)) for i in range(8)]
        acc = [[bank[0], bank[1]], [bank[2], bank[3]]]
        tp = [bank[4], bank[5]]
        sm = [bank[6], bank[7]]
        x_p = [bank[2], bank[3]]
        info_p = bank[5]
        gate_p = bank[4][:, 0:CT * E]
        pos_p = bank[4][:, CT * E:2 * CT * E]
        cnt_p = bank[0][:, 0:E]
        sel_p = bank[1][:, 0:2 * TILES].rearrange("p (a j) -> p a j", a=2)

        def token_bank(c, i):
            return (sm + acc[c % 2])[i]

        up_p = bank[0:4]
        heT_p = bank[4:6]
        y_p = bank[6]
        xe_p = bank[7]

        s_const = sem("s_const")
        s_zero = sem("s_zero")
        s_x = [sem(f"s_x_in{g}") for g in range(NC)]
        s_w = sem("s_w")
        s_adj = [sem("s_adj_even"), sem("s_adj_odd")]
        s_pool = sem("s_pool_own")
        s_alone = sem("s_alone")
        s_dve = sem("s_dve_own")
        s_sqrt = sem("s_sqrt")
        s_var = sem("s_var")
        s_xn = sem("s_xn")
        s_xtp = sem("s_xT_psum")
        s_xt = sem("s_xT")
        s_zp = sem("s_z_psum")
        s_zhi = sem("s_z_hi")
        s_zlo = sem("s_z_lo")
        s_tp = sem("s_adjT_psum")
        s_hi = sem("s_ring_hi")
        s_lo = sem("s_ring_lo")
        s_adjT = sem("s_adjT")
        s_mm = sem("s_adj_products")
        s_h = sem("s_hT")
        s_z2p = sem("s_z2_psum")
        s_z2 = sem("s_z2")
        s_up = sem("s_u_psum")
        s_th = sem("s_tanh")
        s_xres = sem("s_x_res")
        s_x1 = sem("s_x1")
        s_xn1 = sem("s_xn1")
        s_x1st = sem("s_x1_stored")
        s_xn1st = sem("s_xn1_stored")
        s_gate = sem("s_gate_psum")
        s_bf = sem("s_bf_parts")
        s_dlt = sem("s_gap")
        s_idxf = sem("s_choices")
        s_exp = sem("s_exp")
        s_m = sem("s_chosen")
        s_pos = sem("s_pos_psum")
        s_oh = sem("s_onehots")
        s_mask = sem("s_slot_mask")
        s_ohw = sem("s_weighted_onehots")
        s_inf = sem("s_info_mm")
        s_qs = sem("s_slot_of_choice")
        s_te = sem("s_tile_experts")
        s_whi = sem("s_expert_w_hi")
        s_cnt = sem("s_counts_psum")
        s_sel = sem("s_select")
        s_selp = sem("s_slots_psum")
        s_slots = sem("s_slots")

        s_raw = [sem(f"s_raw{i}") for i in range(3)]
        s_ew = sem("s_expert_w")
        s_xg = [sem(f"s_xg{i}") for i in range(YR)]
        s_xs = sem("s_xs")
        s_xep = sem("s_xe_psum")
        s_xehi = sem("s_xe_hi")
        s_xelo = sem("s_xe_lo")
        s_ab = sem("s_up_psum")
        s_sil = sem("s_silu")
        s_he = sem("s_he")
        s_hep = sem("s_heT_psum")
        s_hehi = sem("s_heT_hi")
        s_helo = sem("s_heT_lo")
        s_yp = sem("s_y_psum")
        s_y = sem("s_y")
        s_sc = sem("s_y_added")

        SLOTS = [NT + (7 if c == NC - 2 else 2) for c in range(NC)]
        HOT = [[NT + k for k in ((10, 10, 11, 11, 12, 12, 13, 13) if c == NC - 2 else (3, 4, 6, 7, 9, 10, 12, 13))]
               for c in range(NC)]
        STEPS = HOT[-1][-1] + 2
        S1 = NC * NT

        block = ctx.enter_context(nc.Block())

        def static(v):
            return isinstance(v, int)

        def expert_load(sp, e, n):
            w = (EW1, EW3, EW2)[n]
            k = (KD, KD, KH)[n]
            one = w[bass.ds(e, 1), :, :].rearrange("o (k p) d -> p (o k) d", k=k)
            sp.dma_start(w_raw[:, n, :].rearrange("p (k d) -> p k d", k=k), one).then_inc(s_raw[n], 16)

        def ew_part(buf, n, lo):
            o = buf * EWS
            if n == 2:
                return ew[:, o + 8 * H + 2 * H * lo:o + 8 * H + 2 * H * (lo + 1)]
            v = ew[:, o + 4 * H * lo:o + 4 * H * (lo + 1)].rearrange("p (k d) -> p k d", k=KD)
            return v[:, :, n * H:(n + 1) * H]

        def raw_part(n):
            raw = w_raw[:, n, :]
            return raw if n == 2 else raw.rearrange("p (k d) -> p k d", k=KD)

        def plan_of(engine, j):
            v = engine.value_load(te_i[0:1, bass.ds(j, 1)], min_val=0, max_val=12 * E * E - 1)
            return v % E, v // E % E, v // (E * E) % 4, v // (4 * E * E)

        def refill(engine, plan, n, third):
            e, _, _, fill = plan
            for buf in range(2):
                with engine.If(fill == buf + 1):
                    third(e + 1, buf, n)

        @block.sync
        def _(sp):
            xv = x.rearrange("(t p) d -> p t d", p=P)
            adj_rows = adj.rearrange("(t p) n -> t p n", p=P)
            def x_load(g):
                sp.dma_start(x_in[:, CT * g:CT * (g + 1), :], xv[:, CT * g:CT * (g + 1), :]).then_inc(s_x[g], 16)

            x_load(0)
            for i, w in enumerate((W1, W3, Wf)):
                sp.dma_start(Wg[:, i, :, :], w.rearrange("(k p) d -> p k d", p=P)).then_inc(s_w, 16)
            for i, b in enumerate((b1, b3)):
                sp.dma_start(bT[:, i, :], b.rearrange("(k p) -> p k", p=P),
                             allow_slow_non_contiguous=True).then_inc(s_w, 16)
            for i in range(2):
                sp.dma_start(bf_in[i:i + 1, :], bf.rearrange("(o d) -> o d", o=1)).then_inc(s_w, 16)
            sp.dma_start(gw[:, :, :], gate_w.rearrange("(k p) e -> p k e", p=P)).then_inc(s_w, 16)
            x_load(1)
            for t in range(NT):
                if t >= 2:
                    sp.wait_ge(s_adj[t % 2], 16 * (t // 2))
                if t in (2, 4):
                    x_load(1 + t // 2)
                if t == NT - 2:
                    sp.wait_ge(s_zp, NT)
                sp.dma_start(adj_s[:, t, :], adj_rows[t, :, :]).then_inc(s_adj[t % 2], 16)
            def residual(c):
                sp.dma_start(x_res[:, :, :], xv[:, CT * c:CT * (c + 1), :]).then_inc(s_xres, 16)

            sp.wait_ge(s_zlo, NT + CT)
            residual(0)
            ov = out[0:N, :].rearrange("(t p) d -> p t d", p=P)
            tv = table[0:N, :].rearrange("(t p) d -> p t d", p=P)
            for c in range(NC):
                sp.wait_ge(s_x1, CT * (c + 1))
                sp.dma_start(ov[:, CT * c:CT * (c + 1), :], x1[:, :, :]).then_inc(s_x1st, 16)
                sp.wait_ge(s_xn1, CT * (c + 1))
                sp.dma_start(tv[:, CT * c:CT * (c + 1), :], xn1[:, :, :]).then_inc(s_xn1st, 16)
                if c + 1 < NC:
                    sp.wait_ge(s_xn1st, 16 * (c + 1))
                    sp.wait_ge(s_xtp, NT + CT * (c + 1))
                    residual(c + 1)
                if c == 0:
                    for n in range(3):
                        expert_load(sp, 0, n)
                if c == NC - 2:
                    for n in range(3):
                        sp.wait_ge(s_ew, n + 1)
                        expert_load(sp, 1, n)
            with sp.Fori(2, E) as e:
                for n in range(3):
                    sp.wait_ge(s_ew, 3 * (e - 1) + n + 1)
                    expert_load(sp, e, n)

        @block.gpsimd
        def _(pool):
            own = [0]

            def settle(ins):
                own[0] += 1
                ins.then_inc(s_pool, 1)
                pool.wait_ge(s_pool, own[0])

            settle(nc.gpsimd.memset(ident[:, :], 0.0))
            nc.gpsimd.affine_select(out=ident[:, :], in_=ident[:, :], compare_op=ALU.not_equal, fill=1.0, base=0,
                                    pattern=[[-1, P]], channel_multiplier=1).then_inc(s_const, 1)
            nc.gpsimd.memset(zero_rows[:, :], 0.0).then_inc(s_const, 1)
            settle(nc.gpsimd.memset(ones_b[:, :], 1.0))
            settle(nc.gpsimd.affine_select(out=tri[:, :], in_=ones_b[:, :], compare_op=ALU.is_gt, fill=0.0, base=0,
                                           pattern=[[1, P]], channel_multiplier=-1))
            nc.gpsimd.iota(iota[:, :], pattern=[[1, P]], base=0, channel_multiplier=0,
                           allow_small_or_imprecise_dtypes=True)
            nc.gpsimd.iota(pcol[:, :], pattern=[[0, 1]], base=0, channel_multiplier=1,
                           allow_small_or_imprecise_dtypes=True)
            nc.gpsimd.iota(vcol[:, :], pattern=[[-P, NT]], base=N, channel_multiplier=-1,
                           allow_small_or_imprecise_dtypes=True)
            settle(nc.gpsimd.memset(m_run[:, :, :], 0.0))
            settle(nc.gpsimd.memset(eq_q[:, :], 1.0))
            settle(nc.gpsimd.affine_select(out=eq_q[:, :], in_=eq_q[:, :], compare_op=ALU.is_ge, fill=0.0, base=0,
                                           pattern=[[-NT, E]], channel_multiplier=1))
            settle(nc.gpsimd.affine_select(out=eq_q[:, :], in_=eq_q[:, :], compare_op=ALU.is_ge, fill=0.0,
                                           base=NT - 1, pattern=[[NT, E]], channel_multiplier=-1)
                   )
            settle(nc.gpsimd.tensor_copy(kq[:, :], pcol[:, :]))
            for e in range(1, E):
                m = nc.gpsimd.tensor_scalar(std[:, 0:1], pcol[:, :], float(NT * e), float(-NT), ALU.is_ge, ALU.mult)
                settle(m)
                settle(nc.gpsimd.tensor_tensor(kq[:, :], kq[:, :], std[:, 0:1], ALU.add))
            nc.gpsimd.memset(std[:, :], 0.0).then_inc(s_const, 1)

            def split(e, n):
                pool.wait_ge(s_raw[n], 16 * (e + 1))
                nc.gpsimd.tensor_scalar(ew_part(e, n, 0), raw_part(n), 1.0, 0.0, ALU.mult, ALU.add).then_inc(s_whi, 1)
                pool.wait_ge(s_whi, 3 * e + n + 1)
                nc.gpsimd.tensor_tensor(ew_part(e, n, 1), raw_part(n), ew_part(e, n, 0).bitcast(F32),
                                        ALU.subtract).then_inc(s_ew, 1)

            pool.wait_ge(s_lo, S1 + 2 * NT)
            split(0, 0)
            split(0, 1)
            pool.wait_ge(s_lo, S1 + 3 * NT)
            split(0, 2)
            pool.wait_ge(s_lo, 2 * S1)
            for n in range(3):
                split(1, n)

            pool.wait_ge(s_slots, 1)
            pool.wait_ge(s_zero, 32)
            pool.wait_ge(s_xn1st, 16 * NC)
            pool.wait_ge(s_x1st, 16 * NC)
            for j in range(TILES):
                if j >= YR:
                    pool.wait_ge(s_xg[j % YR], 16 * (j // YR))
                nc.gpsimd.indirect_dma_start(
                    out=xg[:, j, :], out_offset=None, in_=table[:, :],
                    in_offset=bass.IndirectOffsetOnAxis(ap=idx[:, j:j + 1], axis=0),
                    bounds_check=N + P - 1).then_inc(s_xg[j % YR], 16)

            def wait_now(which, value):
                pool.wait_ge(which, value)
                pool.sem_inc(s_alone, 1)

            def add_rows(j, u):
                wait_now(s_y, j + 1)
                if not (static(j) and j == 0):
                    wait_now(s_sc, 16 * j)
                nc.gpsimd.indirect_dma_start(
                    out=out[:, :], out_offset=bass.IndirectOffsetOnAxis(ap=idx_st[:, u, :], axis=0),
                    in_=y_st[:, u, :], in_offset=None, bounds_check=N + P - 1,
                    compute_op=ALU.add).then_inc(s_sc, 16)

            for u in range(YR):
                add_rows(u, u)
            pool.wait_ge(s_te, 1)
            with nc.gpsimd.Fori(1, TILES // YR) as i:
                for u in range(YR):
                    j = i * YR + u
                    with nc.gpsimd.If(plan_of(nc.gpsimd, j)[2] == 1):
                        add_rows(j, u)
            for u in range(YR):
                pool.wait_ge(s_xg[u], 16 * (TILES // YR))
            total = nc.gpsimd.value_load(te_i[0:1, TILES + 1:TILES + 2], min_val=E, max_val=TILES)
            pool.wait_ge(s_sc, 16 * total)

        @block.scalar
        def _(act):
            act.wait_ge(s_const, 2)
            act.dma_start(table[N:N + P, :], zero_rows[:, :]).then_inc(s_zero, 16)
            act.dma_start(out[N:N + P, :], zero_rows[:, :]).then_inc(s_zero, 16)

            def roots(n):
                act.wait_ge(s_var, n)
                nc.scalar.activation(std[:, :], mv[:, :, 1], ACT.Sqrt).then_inc(s_sqrt, 1)

            def x_T(t):
                act.wait_ge(s_xtp, t + 1)
                if t >= 2:
                    act.wait_ge(s_zp, t - 1)
                nc.scalar.copy(xT[:, t % 2, :, :], x_p[t % 2][:, 0:D].rearrange("p (k n) -> p k n", k=KD)
                               ).then_inc(s_xt, 1)

            def z1_hi(t):
                act.wait_ge(s_zp, t + 1)
                nc.scalar.copy(Z[:, 0, t, :], sm[t % 2][:, 0:D]).then_inc(s_zhi, 1)

            def hi_of_block(s):
                layer, c, jb = s // S1, s % S1 // NT, s % NT
                blk = adj_s[:, CT * c:CT * (c + 1), jb * P:(jb + 1) * P]
                dst = ring[:, s % RING, 0, :].rearrange("p (i n) -> p i n", i=CT)
                if s >= RING:
                    act.wait_ge(s_mm, s - RING + 1)
                if layer == 0:
                    act.wait_ge(s_tp, s + 1)
                    src = tp[s % 2][:, :].rearrange("p (i n) -> p i n", i=CT)
                    nc.scalar.copy(dst, src).then_inc(s_hi, 1)
                    nc.scalar.copy(blk, src).then_inc(s_adjT, 1)
                else:
                    nc.scalar.copy(dst, blk).then_inc(s_hi, 1)

            def hidden(layer, c):
                n = layer * NC + c
                act.wait_ge(s_mm, NT * (n + 1))
                if layer == 0 and c == 0:
                    act.wait_ge(s_zero, 32)
                    act.wait_ge(s_bf, 1)
                if n >= 2:
                    if n - 2 < NC:
                        act.wait_ge(s_z2p, CT * (n - 1))
                    else:
                        act.wait_ge(s_up, CT * (n - 1 - NC))
                for f in range(KD):
                    last = nc.scalar.activation(hT[:, n % 2, f, :], acc[n % 2][f][:, :], ACT.Relu,
                                                bias=bT[:, layer, f:f + 1])
                last.then_inc(s_h, 1)

            def z_hi(t):
                act.wait_ge(s_z2, t + 1)
                act.wait_ge(s_mm, S1 - NT + t + 1)
                nc.scalar.copy(Z[:, 0, t, :], z2[:, t, :]).then_inc(s_zhi, 1)

            def token_work(c, k):
                if k in (3, 4):
                    for i in (2 * k - 6, 2 * k - 5):
                        act.wait_ge(s_up, CT * c + i + 1)
                        if c >= 1:
                            act.wait_ge(s_x1st, 16 * c)
                        nc.scalar.activation(x1[:, i, :], token_bank(c, i)[:, 0:D], ACT.Tanh).then_inc(s_th, 1)
                if k == 7:
                    roots(NC + c + 1)
                if k in (10, 11):
                    for i in (2 * k - 20, 2 * k - 19):
                        act.wait_ge(s_xtp, NT + CT * c + i + 1)
                        nc.scalar.copy(xT[:, i, :, :],
                                       token_bank(c, i)[:, 0:D].rearrange("p (k n) -> p k n", k=KD)).then_inc(s_xt, 1)
                if k == NT:
                    act.wait_ge(s_dlt, c + 1)
                    nc.scalar.activation(ex[:, :], dlt[:, :], ACT.Exp).then_inc(s_exp, 1)
                for n in range(2 * CT):
                    if k == HOT[c][n] + 1:
                        m = 2 * CT * c + n
                        act.wait_ge(s_mask, m + 1)
                        for a in range(2):
                            last = nc.scalar.activation(oh_s[:, m % 2, (a + 1) * P:(a + 2) * P], oh_m[:, m % 2, :],
                                                        ACT.Copy, scale=whi[:, a, n:n + 1].bitcast(F32))
                        last.then_inc(s_ohw, 1)

            roots(1)
            x_T(0)
            roots(2)
            x_T(1)
            z1_hi(0)
            for s in range(2 * S1):
                layer, c, jb = s // S1, s % S1 // NT, s % NT
                if s == S1:
                    act.wait_ge(s_adjT, S1)
                hi_of_block(s)
                if s < NT - 1:
                    if s < NT - 2:
                        x_T(s + 2)
                    z1_hi(s + 1)
                if s in (2, 6):
                    roots(3 + s // 6)
                if jb == 1 and s > NT:
                    n = s // NT - 1
                    hidden(n // NC, n % NC)
                if layer == 0 and c == NC - 1 and 2 <= jb < NT - CT + 2:
                    z_hi(jb - 2)
                if layer == 1 and c == 0 and 5 <= jb < 5 + CT:
                    z_hi(NT - CT + jb - 5)
                if layer == 1 and c >= 2:
                    token_work(c - 2, NT + jb)
                if layer == 1 and c >= 1:
                    token_work(c - 1, jb)
            hidden(1, NC - 1)
            for k in range(NT):
                token_work(NC - 2, NT + k)
                token_work(NC - 1, k)
            for k in range(NT, STEPS):
                token_work(NC - 1, k)
            act.wait_ge(s_exp, NC)
            nc.scalar.activation(dlt[:, :], ex[:, :], ACT.Silu).then_inc(s_alone, 1)

            def xe_hi(j):
                act.wait_ge(s_xep, j + 1)
                if not (static(j) and j == 0):
                    act.wait_ge(s_ab, 2 * j)
                nc.scalar.copy(xeT[:, 0, :, :], xe_p[:, 0:D].rearrange("p (k n) -> p k n", k=KD)).then_inc(s_xehi, 1)

            def y_out(j, u):
                act.wait_ge(s_yp, j + 1)
                if not static(j) or j >= YR:
                    act.wait_ge(s_sc, 16 * (j - YR + 1))
                nc.scalar.copy(idx_st[:, u, :], idx[:, bass.ds(j, 1)])
                nc.scalar.activation(y_st[:, u, :], y_p[:, 0:D], ACT.Copy,
                                     scale=wt[:, bass.ds(j, 1)]).then_inc(s_y, 1)

            def third_hi(e, buf, n):
                act.wait_ge(s_raw[n], 16 * (e + 1))
                nc.scalar.copy(ew_part(buf, n, 0), raw_part(n)).then_inc(s_whi, 1)

            def tile(j, u, plan=None):
                for h in range(2):
                    if plan:
                        refill(nc.scalar, plan, h, third_hi)
                    act.wait_ge(s_ab, 2 * j + h + 1)
                    if not (static(j) and j == 0):
                        act.wait_ge(s_he, 2 * j + h - 1)
                    nc.scalar.activation(sil[:, h, :], up_p[h][:, :], ACT.Silu).then_inc(s_sil, 1)
                if not (static(j) and j == TILES - 1):
                    xe_hi(j + 1)
                if not (static(j) and j == 0):
                    y_out(j - 1, (u - 1) % YR)
                for h in range(2):
                    act.wait_ge(s_hep, 2 * j + h + 1)
                    nc.scalar.copy(heT[:, 0, CT * h:CT * (h + 1), :],
                                   heT_p[h][:, :].rearrange("p (k n) -> p k n", k=CT)).then_inc(s_hehi, 1)

            def guarded(j, u):
                plan = plan_of(nc.scalar, j)
                with nc.scalar.If(plan[2] == 1):
                    tile(j, u, plan)
                with nc.scalar.If(plan[2] == 2):
                    y_out(j - 1, (u - 1) % YR)
                refill(nc.scalar, plan, 2, third_hi)

            xe_hi(0)
            act.wait_ge(s_te, 1)
            tile(0, 0)
            act.wait_ge(s_ew, 6)
            for u in range(1, YR):
                plan = plan_of(nc.scalar, u)
                tile(u, u, plan)
                refill(nc.scalar, plan, 2, third_hi)
            with act.Fori(1, TILES // YR) as i:
                for u in range(YR):
                    guarded(i * YR + u, u)
            with nc.scalar.If(plan_of(nc.scalar, TILES)[2] == 2):
                y_out(TILES - 1, YR - 1)

        @block.vector
        def _(dve):
            own = [0]

            def settle(ins):
                own[0] += 1
                ins.then_inc(s_dve, 1)
                dve.wait_ge(s_dve, own[0])

            def stats_of(src, tiles):
                for i in tiles:
                    last = nc.vector.bn_stats(stats[:, i, :], src(i))
                settle(last)

            def spread():
                for i in range(CT):
                    last = nc.vector.bn_aggr(mv[:, i, :], stats[:, i, :])
                settle(last)
                nc.vector.tensor_scalar(mv[:, :, 1], mv[:, :, 1], EPS, None, ALU.add).then_inc(s_var, 1)

            def roots(n):
                dve.wait_ge(s_sqrt, n)
                settle(nc.vector.reciprocal(rstd[:, :], std[:, :]))

            def x_norm(g):
                dve.wait_ge(s_x[g], 16)
                stats_of(lambda i: x_in[:, CT * g + i, :], range(CT))
                spread()
                roots(g + 1)
                for i in range(CT):
                    v = x_in[:, CT * g + i, :]
                    last = nc.vector.tensor_scalar(v, v, mv[:, i, 0:1], rstd[:, i:i + 1], ALU.subtract, ALU.mult)
                last.then_inc(s_xn, 1)

            def z1_lo(t):
                dve.wait_ge(s_zhi, t + 1)
                nc.vector.tensor_tensor(Z[:, 1, t, :], sm[t % 2][:, 0:D], Z[:, 0, t, :].bitcast(F32),
                                        ALU.subtract).then_inc(s_zlo, 1)

            def lo_of_block(s):
                layer, c, jb = s // S1, s % S1 // NT, s % NT
                if layer == 0:
                    dve.wait_ge(s_adjT, s + 1)
                else:
                    dve.wait_ge(s_hi, s + 1)
                hi = ring[:, s % RING, 0, :].bitcast(F32).rearrange("p (i n) -> p i n", i=CT)
                lo = ring[:, s % RING, 1, :].rearrange("p (i n) -> p i n", i=CT)
                src = adj_s[:, CT * c:CT * (c + 1), jb * P:(jb + 1) * P]
                nc.vector.tensor_tensor(lo, src, hi, ALU.subtract).then_inc(s_lo, 1)

            def z_lo(t):
                dve.wait_ge(s_zhi, NT + t + 1)
                nc.vector.tensor_tensor(Z[:, 1, t, :], z2[:, t, :], Z[:, 0, t, :].bitcast(F32),
                                        ALU.subtract).then_inc(s_zlo, 1)

            def z2_out(t):
                dve.wait_ge(s_z2p, t + 1)
                nc.vector.tensor_copy(z2[:, t, :], sm[t % 2][:, 0:D]).then_inc(s_z2, 1)

            def bc(v, n):
                return v.unsqueeze(len(v.shape)).to_broadcast(list(v.shape) + [n])

            def one_hot(c, n):
                m = 2 * CT * c + n
                t = CT * c + n % CT
                if n == 0:
                    dve.wait_ge(s_qs, c + 1)
                if m >= 2:
                    dve.wait_ge(s_inf, m - 1)
                nc.vector.tensor_scalar(oh_q[:, m % 2, :], iota[:, :], qf[:, n:n + 1], None, ALU.is_equal)
                nc.vector.tensor_scalar(oh_m[:, m % 2, :], iota[:, :], sf[:, n:n + 1], None,
                                        ALU.is_equal).then_inc(s_mask, 1)
                nc.vector.tensor_scalar(oh_s[:, m % 2, 0:P], iota[:, :], sf[:, n:n + 1], vcol[:, t:t + 1],
                                        ALU.is_equal, ALU.mult).then_inc(s_oh, 1)

            def token_work(c, k):
                for i in {4: (0, 1), 5: (2,), 6: (3,)}.get(k, ()):
                    dve.wait_ge(s_th, CT * c + i + 1)
                    dve.wait_ge(s_xres, 16 * (c + 1))
                    nc.vector.tensor_tensor(x1[:, i, :], x1[:, i, :], x_res[:, i, :], ALU.add).then_inc(s_x1, 1)
                    dve.wait_ge(s_x1, CT * c + i + 1)
                    stats_of(lambda i: x1[:, i, :], [i])
                if k == 6:
                    spread()
                if k == 8:
                    roots(NC + c + 1)
                if k in (8, 9):
                    for i in (2 * k - 16, 2 * k - 15):
                        nc.vector.tensor_scalar(xn1[:, i, :], x1[:, i, :], mv[:, i, 0:1], rstd[:, i:i + 1],
                                                ALU.subtract, ALU.mult).then_inc(s_xn1, 1)
                if k == NT - 2:
                    dve.wait_ge(s_gate, CT * (c + 1))
                    g = gate_p.rearrange("p (i e) -> p i e", e=E)
                    for i in range(CT):
                        last = nc.vector.max(out=m8[:, i, :], in_=g[:, i, :])
                    settle(last)
                    for i in range(CT):
                        last = nc.vector.max_index(out=ix8[:, i, :], in_max=m8[:, i, :], in_values=g[:, i, :])
                    settle(last)
                    nc.vector.tensor_tensor(dlt[:, :], m8[:, :, 1], m8[:, :, 0], ALU.subtract).then_inc(s_dlt, 1)
                    nc.vector.tensor_copy(idxf[:, :, :], ix8[:, :, 0:2].rearrange("p i k -> p k i")).then_inc(s_idxf, 1)
                if k == NT - 1:
                    dve.wait_ge(s_idxf, c + 1)
                    io = iota[:, 0:E].unsqueeze(1).to_broadcast([P, 2 * CT, E])
                    ohv = oh[:, :, :, :].rearrange("p k i e -> p (k i) e")
                    settle(nc.vector.tensor_tensor(ohv, io, bc(idxf.rearrange("p k i -> p (k i)"), E), ALU.is_equal))
                    if c >= 1:
                        settle(nc.vector.tensor_copy(m_run[:, 0, :], m_run[:, CT, :]))
                    mb = m_bf[:, 0, :].rearrange("p (i e) -> p i e", e=E)
                    settle(nc.vector.tensor_tensor(mb, oh[:, 0, :, :], oh[:, 1, :, :], ALU.add))
                    for i in range(CT):
                        settle(nc.vector.tensor_tensor(m_run[:, i + 1, :], m_run[:, i, :], mb[:, i, :], ALU.add))
                    nc.vector.tensor_copy(m_bf[:, 2, 0:E], m_run[:, CT, :])
                    nc.vector.tensor_copy(m_bf[:, 1, :].rearrange("p (i e) -> p i e", e=E),
                                          m_run[:, 0:CT, :]).then_inc(s_m, 1)
                if k == SLOTS[c]:
                    dve.wait_ge(s_pos, c + 1)
                    for k2 in range(2):
                        last = nc.vector.tensor_tensor(ohpos[:, k2, :, :], oh[:, k2, :, :],
                                                       pos_p.rearrange("p (i e) -> p i e", e=E), ALU.mult)
                    settle(last)
                    settle(nc.vector.tensor_reduce(posk[:, :, :], ohpos[:, :, :, :], AX.X, ALU.add))
                    dve.wait_ge(s_exp, c + 1)
                    nc.vector.tensor_scalar(wk[:, 1, :], ex[:, :], 1.0, None, ALU.add)
                    settle(nc.vector.scalar_tensor_tensor(
                        out=gsl[:, :], in0=idxf.rearrange("p k i -> p (k i)"), scalar=float(N),
                        in1=posk.rearrange("p k i -> p (k i)"), op0=ALU.mult, op1=ALU.add))
                    shift = P.bit_length() - 1
                    nc.vector.reciprocal(wk[:, 0, :], wk[:, 1, :])
                    nc.vector.tensor_scalar(qi[:, :], gsl[:, :], shift, None, ALU.logical_shift_right)
                    settle(nc.vector.tensor_scalar(si[:, :], gsl[:, :], P - 1, None, ALU.bitwise_and))
                    nc.vector.tensor_tensor(wk[:, 1, :], ex[:, :], wk[:, 0, :], ALU.mult)
                    nc.vector.tensor_copy(qf[:, :], qi[:, :])
                    settle(nc.vector.tensor_copy(sf[:, :], si[:, :]))
                    wkf = wk.rearrange("p k i -> p (k i)")
                    settle(nc.vector.tensor_copy(whi[:, 0, :], wkf))
                    nc.vector.tensor_tensor(whi[:, 1, :], wkf, whi[:, 0, :].bitcast(F32),
                                            ALU.subtract).then_inc(s_qs, 1)
                for n in range(2 * CT):
                    if k == HOT[c][n]:
                        one_hot(c, n)

            dve.wait_ge(s_const, 3)
            x_norm(0)
            x_norm(1)
            dve.wait_ge(s_w, 8 * 16)
            sign = bf_sign[:, :]
            nc.vector.tensor_scalar(one_rows[:, :], iota[0:2, :], 0.0, 1.0, ALU.mult, ALU.add)
            nc.vector.tensor_scalar(sign, pcol[0:2, :], -2.0, 1.0, ALU.mult, ALU.add)
            settle(nc.vector.tensor_copy(bf_hi[:, :], bf_in[:, :]))
            settle(nc.vector.tensor_scalar(bf_hi[:, :], bf_hi[:, :].bitcast(F32), sign, None, ALU.mult))
            nc.vector.scalar_tensor_tensor(out=bf_parts[:, :], in0=bf_in[:, :], scalar=pcol[0:2, :],
                                           in1=bf_hi[:, :].bitcast(F32), op0=ALU.mult, op1=ALU.add).then_inc(s_bf, 1)
            z1_lo(0)
            for s in range(2 * S1):
                layer, c, jb = s // S1, s % S1 // NT, s % NT
                if s == S1:
                    dve.wait_ge(s_adjT, S1)
                lo_of_block(s)
                if s < NT - 1:
                    z1_lo(s + 1)
                if s in (2, 6):
                    x_norm(2 + s // 6)
                if layer == 0 and c >= 1 and jb in (3, 4):
                    z2_out(CT * (c - 1) + 2 * jb - 6)
                    z2_out(CT * (c - 1) + 2 * jb - 5)
                if layer == 1 and c == 0 and jb in (3, 4):
                    z2_out(NT - CT + 2 * jb - 6)
                    z2_out(NT - CT + 2 * jb - 5)
                if layer == 0 and c == NC - 1 and 2 <= jb < NT - CT + 2:
                    z_lo(jb - 2)
                if layer == 1 and c == 0 and 5 <= jb < 5 + CT:
                    z_lo(NT - CT + jb - 5)
                if layer == 1 and c >= 2:
                    token_work(c - 2, NT + jb)
                if layer == 1 and c >= 1:
                    token_work(c - 1, jb)
            for k in range(NT):
                token_work(NC - 2, NT + k)
                token_work(NC - 1, k)
            for k in range(NT, STEPS):
                token_work(NC - 1, k)

            dve.wait_ge(s_cnt, 1)
            settle(nc.vector.tensor_scalar(cnt_i[:, :], cnt_p, float(P - 1), None, ALU.add))
            settle(nc.vector.tensor_scalar(cnt_i[:, :], cnt_i[:, :], P.bit_length() - 1, None,
                                           ALU.logical_shift_right))
            settle(nc.vector.tensor_copy(cnt[:, :], cnt_i[:, :]))
            settle(nc.vector.tensor_scalar(tl[:, 1, :], cnt[:, :], 1.0, None, ALU.max))
            settle(nc.vector.memset(cnt[:, :], 1.0))
            settle(nc.vector.tensor_tensor_scan(end[:, :], cnt[:, :], tl[:, 1, :], 0.0, ALU.mult, ALU.add))
            settle(nc.vector.tensor_tensor(tl[:, 0, :], end[:, :], tl[:, 1, :], ALU.subtract))
            tq = tmp_j[:, 0:2 * E].rearrange("p (a e) -> p a e", a=2)
            for a in range(2):
                last = nc.vector.tensor_tensor(tq[:, a, :], tl[:, a, :], eq_q[:, :], ALU.mult)
            settle(last)
            settle(nc.vector.tensor_reduce(sq[:, :], tq, AX.X, ALU.add))
            settle(nc.vector.tensor_scalar(sq[:, 0:1], sq[:, 0:1], kq[:, :], 1.0, ALU.add, ALU.add))
            settle(nc.vector.tensor_tensor(sq[:, 1:2], kq[:, :], sq[:, 1:2], ALU.is_lt))
            settle(nc.vector.tensor_scalar(sq[:, 0:1], sq[:, 0:1], sq[:, 1:2], -1.0, ALU.mult, ALU.add))
            settle(nc.vector.tensor_scalar(sel[:, 0:TILES], iota[:, 0:TILES], sq[:, 0:1], None, ALU.is_equal))
            dve.wait_ge(s_inf, 2 * NT)
            nc.vector.tensor_copy(info[:, 0, :], info_p[:, 0:P])
            settle(nc.vector.tensor_copy(info[:, 1, :], info_p[:, P:2 * P]))
            nc.vector.tensor_tensor(info[:, 1, :], info[:, 1, :], info_p[:, 2 * P:3 * P], ALU.add).then_inc(s_sel, 1)
            dve.wait_ge(s_selp, 1)
            pad = tmp_j[:, 640:640 + TILES]
            settle(nc.vector.tensor_scalar(pad, sel_p[:, 0, :], 0.0, pcol[:, :], ALU.is_equal, ALU.mult))
            settle(nc.vector.tensor_tensor(pad, pad, sel_p[:, 0, :], ALU.subtract))
            nc.vector.tensor_scalar(idx[:, :], pad, float(N), None, ALU.add).then_inc(s_slots, 1)
            nc.vector.tensor_copy(wt[:, :], sel_p[:, 1, :])
            TU = TILES + 1
            cmp = tmp_j[0:1, 16:16 + TU * (E - 1)].rearrange("p (j e) -> p j e", e=E - 1)
            te, use, fill, wk_t = (te_f[:, a, :] for a in range(4))
            ej = end[0:1, 0:E - 1].unsqueeze(1).to_broadcast([1, TU, E - 1])
            settle(nc.vector.tensor_tensor(cmp, ej, bc(iota[0:1, 0:TU], E - 1), ALU.is_le))
            nc.vector.tensor_scalar(use, iota[0:1, 0:TU], end[0:1, E - 1:E], None, ALU.is_lt)
            nc.vector.tensor_scalar(wk_t, iota[0:1, 0:TU], end[0:1, E - 1:E], 2.0, ALU.is_equal, ALU.mult)
            settle(nc.vector.tensor_reduce(te, cmp, AX.X, ALU.add))
            nc.vector.tensor_tensor(use, use, wk_t, ALU.add)
            nc.vector.memset(fill[:, 0:1], 0.0)
            settle(nc.vector.tensor_scalar(te_i[:, 0:TU], te, 1.0, None, ALU.add))
            nc.vector.tensor_tensor(fill[:, 1:TU], te[:, 1:TU], te[:, 0:TU - 1], ALU.subtract)
            nc.vector.tensor_scalar(wk_t, te, float(E - 2), None, ALU.is_le)
            settle(nc.vector.tensor_scalar(te_i[:, 0:TU], te_i[:, 0:TU], 1, None, ALU.bitwise_and))
            settle(nc.vector.tensor_tensor(fill, fill, wk_t, ALU.mult))
            settle(nc.vector.tensor_copy(wk_t, te_i[:, 0:TU]))
            settle(nc.vector.scalar_tensor_tensor(out=fill, in0=wk_t, scalar=1.0, in1=fill,
                                                  op0=ALU.add, op1=ALU.mult))
            settle(nc.vector.scalar_tensor_tensor(out=fill, in0=fill, scalar=4.0, in1=use,
                                                  op0=ALU.mult, op1=ALU.add))
            settle(nc.vector.tensor_scalar(fill, fill, float(E), None, ALU.mult))
            settle(nc.vector.tensor_tensor(fill[:, 1:TU], fill[:, 1:TU], te[:, 0:TU - 1], ALU.add))
            settle(nc.vector.scalar_tensor_tensor(out=te_i[:, 0:TU], in0=fill, scalar=float(E), in1=te,
                                                  op0=ALU.mult, op1=ALU.add))
            nc.vector.tensor_copy(te_i[:, TU:TU + 1], end[0:1, E - 1:E]).then_inc(s_te, 1)

            def row_copy(j, u, i):
                dve.wait_ge(s_xg[u], 16 * (i + 1))
                if not (static(j) and j == 0):
                    dve.wait_ge(s_xep, j)
                nc.vector.tensor_copy(xs[:, :], xg[:, bass.ds(j, 1), :].rearrange("p o d -> p (o d)")).then_inc(s_xs, 1)

            def xe_lo(j):
                dve.wait_ge(s_xehi, j + 1)
                nc.vector.tensor_tensor(xeT[:, 1, :, :], xe_p[:, 0:D].rearrange("p (k n) -> p k n", k=KD),
                                        xeT[:, 0, :, :].bitcast(F32), ALU.subtract).then_inc(s_xelo, 1)

            def third_lo(e, buf, n):
                dve.wait_ge(s_whi, 3 * e + n + 1)
                nc.vector.tensor_tensor(ew_part(buf, n, 1), raw_part(n), ew_part(buf, n, 0).bitcast(F32),
                                        ALU.subtract).then_inc(s_ew, 1)

            def tile(j, u, i, plan=None):
                if not (static(j) and j == TILES - 1):
                    row_copy(j + 1, (u + 1) % YR, i + (u + 1) // YR)
                if plan:
                    refill(nc.vector, plan, 0, third_lo)
                for h in range(2):
                    dve.wait_ge(s_sil, 2 * j + h + 1)
                    if not (static(j) and j == 0):
                        dve.wait_ge(s_hep, 2 * j)
                    nc.vector.tensor_tensor(he[:, h * HW:(h + 1) * HW], sil[:, h, :], up_p[2 + h][:, :],
                                            ALU.mult).then_inc(s_he, 1)
                if plan:
                    refill(nc.vector, plan, 1, third_lo)
                if not (static(j) and j == TILES - 1):
                    xe_lo(j + 1)
                for h in range(2):
                    dve.wait_ge(s_hehi, 2 * j + h + 1)
                    nc.vector.tensor_tensor(heT[:, 1, CT * h:CT * (h + 1), :],
                                            heT_p[h][:, :].rearrange("p (k n) -> p k n", k=CT),
                                            heT[:, 0, CT * h:CT * (h + 1), :].bitcast(F32),
                                            ALU.subtract).then_inc(s_helo, 1)

            def guarded(j, u, i):
                plan = plan_of(nc.vector, j)
                with nc.vector.If(plan[2] == 1):
                    tile(j, u, i, plan)
                refill(nc.vector, plan, 2, third_lo)

            dve.wait_ge(s_te, 1)
            row_copy(0, 0, 0)
            xe_lo(0)
            tile(0, 0, 0)
            dve.wait_ge(s_ew, 6)
            for u in range(1, YR):
                plan = plan_of(nc.vector, u)
                tile(u, u, 0, plan)
                refill(nc.vector, plan, 2, third_lo)
            with dve.Fori(1, TILES // YR - 1) as i:
                for u in range(YR):
                    guarded(i * YR + u, u, i)
            for u in range(YR):
                guarded(TILES - YR + u, u, TILES // YR - 1)

        @block.tensor
        def _(pe):
            pe.wait_ge(s_const, 3)
            pe.wait_ge(s_w, 8 * 16)

            def x_T(t):
                pe.wait_ge(s_xn, t // CT + 1)
                if t >= 2:
                    pe.wait_ge(s_xt, t - 1)
                for k in range(KD):
                    last = nc.tensor.transpose(x_p[t % 2][:, k * P:(k + 1) * P], x_in[:, t, k * P:(k + 1) * P],
                                               ident[:, :])
                last.then_inc(s_xtp, 1)

            def z1_rows(t):
                pe.wait_ge(s_xt, t + 1)
                if t >= 2:
                    pe.wait_ge(s_zlo, t - 1)
                for k in range(KD):
                    last = nc.tensor.matmul(sm[t % 2][:, 0:D], xT[:, t % 2, k, :], Wg[:, 0, k, :],
                                            start=(k == 0), stop=(k == KD - 1))
                last.then_inc(s_zp, 1)

            def transpose_block(s):
                c, jb = s // NT, s % NT
                if jb == 0:
                    for par in range(2):
                        pe.wait_ge(s_adj[par], 16 * (CT * (c + 1) // 2))
                if s >= 2:
                    pe.wait_ge(s_adjT, s - 1)
                for i in range(CT):
                    last = nc.tensor.transpose(tp[s % 2][:, i * P:(i + 1) * P],
                                               adj_s[:, CT * c + i, jb * P:(jb + 1) * P], ident[:, :])
                last.then_inc(s_tp, 1)

            def product(s):
                n, jb = s // NT, s % NT
                pe.wait_ge(s_lo, s + 1)
                if n == 0:
                    pe.wait_ge(s_zlo, jb + 1)
                if n == NC:
                    pe.wait_ge(s_zlo, NT + jb + 1)
                if jb == 0 and n >= 2:
                    pe.wait_ge(s_h, n - 1)
                    if n >= NC + 2:
                        pe.wait_ge(s_xt, NT + CT * (n - NC - 1))
                hi, lo = ring[:, s % RING, 0, :], ring[:, s % RING, 1, :]
                for f in range(KD):
                    zh = Z[:, 0, jb, f * P:(f + 1) * P]
                    zl = Z[:, 1, jb, f * P:(f + 1) * P]
                    a = acc[n % 2][f][:, :]
                    nc.tensor.matmul(a, zh, hi, start=(jb == 0), stop=False)
                    nc.tensor.matmul(a, zh, lo, start=False, stop=False)
                    last = nc.tensor.matmul(a, zl, hi, start=False, stop=(jb == NT - 1))
                last.then_inc(s_mm, 1)

            def z2_rows(t):
                c = t // CT
                pe.wait_ge(s_h, c + 1)
                if t >= 2:
                    pe.wait_ge(s_z2, t - 1)
                for k in range(KD):
                    last = nc.tensor.matmul(sm[t % 2][:, 0:D], hT[:, c % 2, k, (t % CT) * P:(t % CT + 1) * P],
                                            Wg[:, 1, k, :], start=(k == 0), stop=(k == KD - 1))
                last.then_inc(s_z2p, 1)

            def slot_map(c, n):
                m = 2 * CT * c + n
                pe.wait_ge(s_oh, m + 1)
                pe.wait_ge(s_ohw, m + 1)
                nc.tensor.matmul(info_p[:, 0:3 * P], oh_q[:, m % 2, :], oh_s[:, m % 2, :], start=(m == 0),
                                 stop=(m == 2 * NT - 1)).then_inc(s_inf, 1)

            def token_work(c, k):
                if k in (2, 3):
                    for i in (2 * k - 4, 2 * k - 3):
                        b = token_bank(c, i)[:, 0:D]
                        pe.wait_ge(s_h, NC + c + 1)
                        if c == 0:
                            pe.wait_ge(s_z2, NT)
                            pe.wait_ge(s_bf, 1)
                        nc.tensor.matmul(b, one_rows[:, :], bf_parts[:, :], start=True, stop=False)
                        for f in range(KD):
                            last = nc.tensor.matmul(b, hT[:, c % 2, f, i * P:(i + 1) * P], Wg[:, 2, f, :],
                                                    start=False, stop=(f == KD - 1))
                        last.then_inc(s_up, 1)
                if k in (9, 10):
                    for i in (2 * k - 18, 2 * k - 17):
                        pe.wait_ge(s_xn1, CT * c + i + 1)
                        for f in range(KD):
                            last = nc.tensor.transpose(token_bank(c, i)[:, f * P:(f + 1) * P],
                                                       xn1[:, i, f * P:(f + 1) * P], ident[:, :])
                        last.then_inc(s_xtp, 1)
                if k in (11, 12):
                    for i in (2 * k - 22, 2 * k - 21):
                        pe.wait_ge(s_xt, NT + CT * c + i + 1)
                        if c >= 1:
                            pe.wait_ge(s_qs, c)
                        for f in range(KD):
                            last = nc.tensor.matmul(gate_p[:, i * E:(i + 1) * E], xT[:, i, f, :], gw[:, f, :],
                                                    start=(f == 0), stop=(f == KD - 1))
                        last.then_inc(s_gate, 1)
                if k == NT:
                    pe.wait_ge(s_m, c + 1)
                    nc.tensor.matmul(pos_p, tri[:, :], m_bf[:, 0, :], start=True, stop=False)
                    nc.tensor.matmul(pos_p, ones_b[:, :], m_bf[:, 1, :], start=False, stop=True).then_inc(s_pos, 1)
                for n in range(2 * CT):
                    if k == HOT[c][n] + 1:
                        slot_map(c, n)

            for t in range(2):
                x_T(t)
            z1_rows(0)
            transpose_block(0)
            transpose_block(1)
            for s in range(2 * S1):
                layer, c, jb = s // S1, s % S1 // NT, s % NT
                if s < NT - 1:
                    if s < NT - 2:
                        x_T(s + 2)
                    z1_rows(s + 1)
                if s + 2 < S1:
                    transpose_block(s + 2)
                product(s)
                if NT <= s < S1 + NT and jb in (2, 3):
                    z2_rows(CT * (s // NT - 1) + 2 * jb - 4)
                    z2_rows(CT * (s // NT - 1) + 2 * jb - 3)
                if layer == 1 and c >= 2:
                    token_work(c - 2, NT + jb)
                if layer == 1 and c >= 1:
                    token_work(c - 1, jb)
            for k in range(NT):
                token_work(NC - 2, NT + k)
                token_work(NC - 1, k)
            token_work(NC - 1, NT)
            nc.tensor.matmul(cnt_p, ones_b[:, :], m_bf[:, 2, 0:E], start=True, stop=True).then_inc(s_cnt, 1)
            for k in range(NT + 1, STEPS):
                token_work(NC - 1, k)
            pe.wait_ge(s_sel, 1)
            for a in range(2):
                last = nc.tensor.matmul(sel_p[:, a, :], info[:, a, :], sel[:, 0:TILES], start=True, stop=True)
            last.then_inc(s_selp, 1)

            def rows_T(j):
                pe.wait_ge(s_xs, j + 1)
                if not (static(j) and j == 0):
                    pe.wait_ge(s_xelo, j)
                for k in range(KD):
                    last = nc.tensor.transpose(xe_p[:, k * P:(k + 1) * P], xs[:, k * P:(k + 1) * P], ident[:, :])
                last.then_inc(s_xep, 1)

            def three(out_ap, k0, k1, stat, w_at):
                for k in range(k0, k1):
                    for sl, wl in ((0, 0), (0, 1), (1, 0)):
                        last = nc.tensor.matmul(out_ap, stat[:, sl, k, :], w_at(k, wl),
                                                start=(k == k0 and sl == wl == 0), stop=(k == k1 - 1 and sl == 1))
                return last

            def up_from(j, buf):
                for h in range(2):
                    if not (static(j) and j == 0):
                        pe.wait_ge(s_he, 2 * j - 1 + h)
                    for m in range(2):
                        o = buf * EWS + m * H + h * HW
                        last = three(up_p[2 * m + h][:, :], 0, KD, xeT,
                                     lambda k, lo: ew[:, o + 4 * H * lo + 2 * H * k:][:, 0:HW])
                    last.then_inc(s_ab, 1)

            def down_from(buf):
                o = buf * EWS + 8 * H
                three(y_p[:, 0:D], 0, KH, heT, lambda k, lo: ew[:, o + 2 * H * lo + D * k:][:, 0:D]).then_inc(s_yp, 1)

            def up(j, e):
                pe.wait_ge(s_ew, 3 * e + 2)
                pe.wait_ge(s_xelo, j + 1)
                side = e % 2
                for buf in range(2):
                    with nc.tensor.If(side == buf):
                        up_from(j, buf)

            def down(j, e):
                pe.wait_ge(s_ew, 3 * e + 3)
                pe.wait_ge(s_helo, 2 * j + 2)
                if not (static(j) and j == 0):
                    pe.wait_ge(s_y, j)
                if static(e):
                    down_from(e % 2)
                    return
                side = e % 2
                for buf in range(2):
                    with nc.tensor.If(side == buf):
                        down_from(buf)

            def hidden_T(j):
                for h in range(2):
                    pe.wait_ge(s_he, 2 * j + h + 1)
                    for k in range(CT):
                        last = nc.tensor.transpose(heT_p[h][:, k * P:(k + 1) * P],
                                                   he[:, (CT * h + k) * P:(CT * h + k + 1) * P], ident[:, :])
                    last.then_inc(s_hep, 1)

            def outputs_before(j, plan):
                with nc.tensor.If(plan[2] > 0):
                    down(j - 1, plan[1])

            def middle(j, plan, last=False):
                outputs_before(j, plan)
                following = plan_of(nc.tensor, j + 1)
                with nc.tensor.If(plan[2] == 1):
                    hidden_T(j)
                with nc.tensor.If(following[2] == 1):
                    up(j + 1, following[0])
                    if last:
                        pe.wait_ge(s_xelo, TILES)
                    else:
                        rows_T(j + 2)
                return following

            rows_T(0)
            pe.wait_ge(s_ew, 2)
            pe.wait_ge(s_xelo, 1)
            up_from(0, 0)
            rows_T(1)
            hidden_T(0)
            pe.wait_ge(s_te, 1)
            up(1, plan_of(nc.tensor, 1)[0])
            rows_T(2)
            with pe.Fori(0, (TILES - 3) // YR) as i:
                plan = plan_of(nc.tensor, i * YR + 1)
                for u in range(YR):
                    plan = middle(i * YR + u + 1, plan)
            plan = middle(TILES - 2, plan_of(nc.tensor, TILES - 2), last=True)
            outputs_before(TILES - 1, plan)
            with nc.tensor.If(plan[2] == 1):
                hidden_T(TILES - 1)
            with nc.tensor.If(plan_of(nc.tensor, TILES)[2] == 2):
                down(TILES - 1, E - 1)
                pe.wait_ge(s_he, 2 * TILES)


_INS = ['x', 'adj', 'L0_gnn_W1', 'L0_gnn_b1', 'L0_gnn_W3', 'L0_gnn_b3', 'L0_gnn_Wf', 'L0_gnn_bf', 'L0_ffn_gate_w',
        'L0_ffn_W1', 'L0_ffn_W2', 'L0_ffn_W3']


def kernel(**inputs):
    import numpy as np
    import concourse.bacc as bacc
    from concourse.bass_utils import run_bass_kernel_spmd

    nc = bacc.Bacc("TRN2", target_bir_lowering=False, num_devices=1)
    arrays, args = {}, []
    for name in _INS:
        a = np.ascontiguousarray(inputs[name])
        arrays[f"in_{name}"] = a
        args.append(nc.dram_tensor(f"in_{name}", a.shape, mybir.dt.from_np(a.dtype), kind="ExternalInput").ap())
    n, d = inputs['x'].shape
    o = nc.dram_tensor("out_0", (n + nc.NUM_PARTITIONS, d), F32, kind="ExternalOutput").ap()
    gnn_and_routed_ffn(nc, *args, o)
    r = run_bass_kernel_spmd(nc, [arrays], core_ids=[0])
    return r.results[0]["out_0"][:n]
```

```python
import concourse.bass as bass
from concourse import mybir
from concourse.alu_op_type import AluOpType as ALU
from contextlib import ExitStack

F32 = mybir.dt.float32
F32R = mybir.dt.float32r
BF16 = mybir.dt.bfloat16
I32 = mybir.dt.int32
U32 = mybir.dt.uint32
ACT = mybir.ActivationFunctionType
AX = mybir.AxisListType


def gnn_and_routed_ffn(nc, x, adj, W1, b1, W3, b3, Wf, bf, gate_w, EW1, EW2, EW3, out):
    P = nc.NUM_PARTITIONS
    N, D = x.shape
    E, _, H = EW1.shape
    KD = D // P
    KH = H // P
    NT = N // P
    CT = 4
    NC = NT // CT
    CW = CT * P
    TOPK = 2
    TILES = (TOPK * N + E * (P - 1)) // P
    EPS = 1e-5
    HW = 512
    RING = 3
    YR = 3
    TURN = 6
    assert TILES % YR == 0 and (TILES - 3) % TURN == 0 and NT * E == P and KD == 2

    table = nc.dram_tensor("ffn_in_rows", (N + P, D), F32).ap()

    ctx = ExitStack()
    with ctx:
        def sem(name):
            return ctx.enter_context(nc.semaphore(name))

        KB = 1024
        arena = ctx.enter_context(nc.sbuf_tensor("arena", [P, 202 * KB // 4], F32))
        base = 16512

        def at(name, shape, dtype, kb):
            return nc.alloc_sbuf_tensor_at(name, shape, dtype, offset=base + int(kb * KB))

        adj_s = at("adj_s", [P, NT, N], F32, 0)
        x_in = at("x_in", [P, NT, D], F32, 112)
        Z = at("Z", [P, 2, NT, D], F32R, 128)
        z2 = at("z2", [P, NT, D], F32, 160)
        W1s = at("W1s", [P, 2, KD, D], F32R, 160)
        xTs = at("xTs", [P, 2, 2, KD, P], F32R, 168)
        x_res = at("x_res", [P, CT, D], F32, 160)
        x1 = at("x1", [P, CT, D], F32, 164)
        xn1 = x_res
        xT = at("xT", [P, CT, KD, P], F32, 168)
        oh_q = at("oh_q", [P, 2, P], F32R, 172)
        oh_s = at("oh_s", [P, 2, 3 * P], F32R, 173)
        zero_rows = at("zero_rows", [P, D], F32, 176)
        bf_in = at("bf_in", [2, D], F32, 177)
        bf_hi = at("bf_hi", [2, D], F32R, 178)
        hT = at("hT", [P, 2, KD, CW], F32, 176)
        hTs = at("hTs", [P, 2, KD, CW], F32R, 176)
        hTf = at("hTf", [P, 2, KD, CW], F32, 176)
        ring = at("ring", [P, RING, 2, CW], F32R, 184)
        Wg = at("Wg", [P, 3, KD, D], F32, 196)
        W3s = at("W3s", [P, 2, KD, D], F32R, 196)
        oh_m = at("oh_m", [P, 2, P], F32, 198)
        route = at("route", [P, KB // 2], F32, 196)
        w_raw = at("w_raw", [P, 3, 2 * H], F32, 0)
        EWS = 12 * H
        ew = at("ew", [P, 2 * EWS], F32R, 24)
        xg = at("xg", [P, TILES, D], F32, 120)
        heT = at("heT", [P, 2, KH, P], F32R, 160)
        he = at("he", [P, H], F32, 168)
        sil = at("sil", [P, 2, HW], F32, 172)
        y_st = at("y_st", [P, YR, D], F32, 176)
        xs = at("xs", [P, D], F32, 179)
        xeT = at("xeT", [P, 2, KD, P], F32R, 184)

        def sb(name, shape, dt):
            return ctx.enter_context(nc.sbuf_tensor(name, shape, dt))

        ident = sb("ident", [P, P], F32)
        iota = sb("iota", [P, P], F32)
        tri = sb("tri", [P, P], BF16)
        ones_b = sb("ones_b", [P, P], BF16)
        bf_parts = sb("bf_parts", [2, D], F32R)
        one_rows = sb("one_rows", [2, P], F32R)
        gw = sb("gw", [P, KD, E], F32)
        bT = sb("bT", [P, 2, KD], F32)
        m_run = sb("m_run", [P, CT + 1, E], F32)
        pcol = sb("pcol", [P, 1], F32)
        idx = sb("idx", [P, TILES], I32)
        wt = sb("wt", [P, TILES], F32)
        idx_st = sb("idx_st", [P, YR, 1], I32)

        used = [0]

        def cut(*shape):
            n = 1
            for s in shape:
                n *= s
            v = route[:, used[0]:used[0] + n]
            used[0] += n
            if len(shape) == 1:
                return v
            names = " ".join("abcd"[:len(shape)])
            return v.rearrange(f"p ({names}) -> p {names}", **dict(zip("abcd", shape)))

        stats = sb("stats", [P, CT, 6], F32)
        mv = sb("mv", [P, CT, 2], F32)
        std = sb("std", [P, CT], F32)
        rstd = sb("rstd", [P, CT], F32)
        m8 = cut(CT, E)
        ix8 = cut(CT, E).bitcast(U32)
        oh = cut(2, CT, E)
        ohpos = cut(2, CT, E)
        idxf = cut(2, CT)
        dlt = cut(CT)
        ex = cut(CT)
        wk = cut(2, CT)
        gsl = cut(2 * CT).bitcast(I32)
        qi = cut(2 * CT).bitcast(I32)
        si = cut(2 * CT).bitcast(I32)
        qf = cut(2 * CT)
        sf = cut(2 * CT)
        posk = cut(2, CT)
        cnt = cut(E)
        cnt_i = cut(E).bitcast(I32)
        tl = cut(2, E)
        end = cut(E)
        sq = cut(2)
        vcol = sb("vcol", [P, NT], F32)
        eq_q = sb("eq_q", [P, E], F32)
        kq = sb("kq", [P, 1], F32)
        bf_sign = sb("bf_sign", [2, 1], F32)
        m_bf = sb("m_bf", [P, 3, CT * E], BF16)
        whi2 = sb("whi2", [P, 2, 2, 2 * CT], F32R)
        info = at("info", [P, 2, P], F32, 184)
        sel = at("sel", [P, P], F32, 185)
        tmp_j = at("tmp_j", [P, 8 * P], F32, 186)
        oh_q2 = at("oh_q2", [P, 2, P], F32R, 190)
        oh_s2 = at("oh_s2", [P, 2, 3 * P], F32R, 191)
        oh_m2 = at("oh_m2", [P, 2, P], F32, 194)
        te_i = sb("te_i", [1, TILES + 2], I32)

        bank = [ctx.enter_context(nc.psum_tensor(f"bank{i}", [P, HW], F32)) for i in range(8)]
        acc = [[bank[0], bank[1]], [bank[2], bank[3]]]
        tp = [bank[4], bank[5]]
        sm = [bank[6], bank[7]]
        x_p = [bank[2], bank[3]]
        info_p = bank[5]
        gate_p = bank[4][:, 0:CT * E]
        pos_p = bank[4][:, CT * E:2 * CT * E]
        cnt_p = bank[0][:, 0:E]
        sel_p = bank[1][:, 0:TILES]
        wt_p = bank[2][:, 0:TILES]

        def token_bank(c, i):
            return (sm + acc[c % 2])[i]

        def oh_slot(c, n):
            m = 2 * CT * c + n
            four = c >= NC - 2
            used = m - 1 if not four or (c == NC - 2 and n < 2) else m - 3
            q, mask, s3 = (oh_q, oh_m, oh_s) if not four or n % 4 < 2 else (oh_q2, oh_m2, oh_s2)
            return q[:, n % 2, :], mask[:, n % 2, :], s3[:, n % 2, :], used

        up_p = bank[0:4]
        heT_p = bank[4:6]
        y_p = bank[6]
        xe_p = bank[7]

        s_const = sem("s_const")
        s_zero = sem("s_zero")
        s_x = [sem(f"s_x_in{g}") for g in range(NC)]
        s_w1 = sem("s_W1_in")
        s_w = sem("s_weights_in")
        s_adj = [sem("s_adj_even"), sem("s_adj_odd")]
        s_pool = sem("s_pool_own")
        s_alone = sem("s_alone")
        s_dve = sem("s_dve_own")
        s_sqrt = sem("s_sqrt")
        s_var = sem("s_var")
        s_xn = sem("s_xn")
        s_xtp = sem("s_xT_psum")
        s_xt = sem("s_xT")
        s_xtlo = sem("s_xT_lo")
        s_w1s = sem("s_W1_split")
        s_zp = sem("s_z_psum")
        s_zhi = sem("s_z_hi")
        s_zlo = sem("s_z_lo")
        s_tp = sem("s_adjT_psum")
        s_hi = sem("s_ring_hi")
        s_lo = sem("s_ring_lo")
        s_adjT = sem("s_adjT")
        s_mm = sem("s_adj_products")
        s_h1 = sem("s_hT_layer1")
        s_h2 = sem("s_hT_layer2")
        s_hlo = sem("s_hT_lo")
        s_w3s = sem("s_W3_split")
        s_z2p = sem("s_z2_psum")
        s_z2 = sem("s_z2")
        s_up = sem("s_u_psum")
        s_th = sem("s_tanh")
        s_xres = sem("s_x_res")
        s_x1 = sem("s_x1")
        s_xn1 = sem("s_xn1")
        s_x1st = sem("s_x1_stored")
        s_xn1st = sem("s_xn1_stored")
        s_gate = sem("s_gate_psum")
        s_bf = sem("s_bf_parts")
        s_dlt = sem("s_gap")
        s_idxf = sem("s_choices")
        s_exp = sem("s_exp")
        s_m = sem("s_chosen")
        s_pos = sem("s_pos_psum")
        s_oh = sem("s_onehots")
        s_mask = sem("s_slot_mask")
        s_ohw = sem("s_weighted_onehots")
        s_inf = sem("s_info_mm")
        s_qs = sem("s_slot_of_choice")
        s_te = sem("s_tile_experts")
        s_whi = sem("s_expert_w_hi")
        s_cnt = sem("s_counts_psum")
        s_sel = sem("s_select")
        s_selp = sem("s_slots_psum")
        s_slots = sem("s_slots")

        s_raw = [sem(f"s_raw{i}") for i in range(3)]
        s_ew = sem("s_expert_w")
        s_xg = [sem(f"s_xg{i}") for i in range(YR)]
        s_xs = sem("s_xs")
        s_xep = sem("s_xe_psum")
        s_xehi = sem("s_xe_hi")
        s_xelo = sem("s_xe_lo")
        s_ab = sem("s_up_psum")
        s_sil = sem("s_silu")
        s_he = sem("s_he")
        s_hep = sem("s_heT_psum")
        s_hehi = sem("s_heT_hi")
        s_helo = sem("s_heT_lo")
        s_yp = sem("s_y_psum")
        s_y = sem("s_y")
        s_sc = sem("s_y_added")

        SLOTS = [NT + (10 if c == NC - 2 else 2) for c in range(NC)]
        HOT = [[NT + k for k in ((12, 12, 12, 12, 16, 16, 16, 16) if c == NC - 2 else (3, 4, 6, 7, 9, 10, 12, 13))]
               for c in range(NC)]
        STEPS = HOT[-1][-1] + 2
        S1 = NC * NT

        block = ctx.enter_context(nc.Block())

        def static(v):
            return isinstance(v, int)

        def expert_load(sp, e, n):
            w = (EW1, EW3, EW2)[n]
            k = (KD, KD, KH)[n]
            one = w[bass.ds(e, 1), :, :].rearrange("o (k p) d -> p (o k) d", k=k)
            sp.dma_start(w_raw[:, n, :].rearrange("p (k d) -> p k d", k=k), one).then_inc(s_raw[n], 16)

        def ew_part(buf, n, lo):
            o = buf * EWS
            if n == 2:
                return ew[:, o + 8 * H + 2 * H * lo:o + 8 * H + 2 * H * (lo + 1)]
            v = ew[:, o + 4 * H * lo:o + 4 * H * (lo + 1)].rearrange("p (k d) -> p k d", k=KD)
            return v[:, :, n * H:(n + 1) * H]

        def raw_part(n):
            raw = w_raw[:, n, :]
            return raw if n == 2 else raw.rearrange("p (k d) -> p k d", k=KD)

        def plan_of(engine, j):
            v = engine.value_load(te_i[0:1, bass.ds(j, 1)], min_val=0, max_val=12 * E * E - 1)
            return v % E, v // E % E, v // (E * E) % 4, v // (4 * E * E)

        def refill(engine, plan, n, third):
            e, _, _, fill = plan
            for buf in range(2):
                with engine.If(fill == buf + 1):
                    third(e + 1, buf, n)

        @block.sync
        def _(sp):
            xv = x.rearrange("(t p) d -> p t d", p=P)
            adj_rows = adj.rearrange("(t p) n -> t p n", p=P)
            def x_load(g):
                sp.dma_start(x_in[:, CT * g:CT * (g + 1), :], xv[:, CT * g:CT * (g + 1), :]).then_inc(s_x[g], 16)

            def weight_load(i, w, done):
                sp.dma_start(Wg[:, i, :, :], w.rearrange("(k p) d -> p k d", p=P)).then_inc(done, 16)

            x_load(0)
            weight_load(0, W1, s_w1)
            for t in range(NT):
                if t >= 2:
                    sp.wait_ge(s_adj[t % 2], 16 * (t // 2))
                if CT <= t < CT + NC - 1:
                    x_load(t - CT + 1)
                if t == CT + NC:
                    weight_load(1, W3, s_w)
                    weight_load(2, Wf, s_w)
                    for i, b in enumerate((b1, b3)):
                        sp.dma_start(bT[:, i, :], b.rearrange("(k p) -> p k", p=P),
                                     allow_slow_non_contiguous=True).then_inc(s_w, 16)
                    for i in range(2):
                        sp.dma_start(bf_in[i:i + 1, :], bf.rearrange("(o d) -> o d", o=1)).then_inc(s_w, 16)
                    sp.dma_start(gw[:, :, :], gate_w.rearrange("(k p) e -> p k e", p=P)).then_inc(s_w, 16)
                if t == NT - 2:
                    sp.wait_ge(s_zp, NT)
                sp.dma_start(adj_s[:, t, :], adj_rows[t, :, :]).then_inc(s_adj[t % 2], 16)
            def residual(c):
                sp.dma_start(x_res[:, :, :], xv[:, CT * c:CT * (c + 1), :]).then_inc(s_xres, 16)

            sp.wait_ge(s_zlo, NT + CT)
            residual(0)
            ov = out[0:N, :].rearrange("(t p) d -> p t d", p=P)
            tv = table[0:N, :].rearrange("(t p) d -> p t d", p=P)
            for c in range(NC):
                sp.wait_ge(s_x1, CT * (c + 1))
                sp.dma_start(ov[:, CT * c:CT * (c + 1), :], x1[:, :, :]).then_inc(s_x1st, 16)
                sp.wait_ge(s_xn1, CT * (c + 1))
                sp.dma_start(tv[:, CT * c:CT * (c + 1), :], xn1[:, :, :]).then_inc(s_xn1st, 16)
                if c + 1 < NC:
                    sp.wait_ge(s_xn1st, 16 * (c + 1))
                    sp.wait_ge(s_xtp, NT + CT * (c + 1))
                    residual(c + 1)
                if c == 0:
                    for n in range(3):
                        expert_load(sp, 0, n)
                if c == NC - 2:
                    for n in range(3):
                        sp.wait_ge(s_ew, n + 1)
                        expert_load(sp, 1, n)
            with sp.Fori(2, E) as e:
                for n in range(3):
                    sp.wait_ge(s_ew, 3 * (e - 1) + n + 1)
                    expert_load(sp, e, n)

        @block.gpsimd
        def _(pool):
            own = [0]

            def settle(ins):
                own[0] += 1
                ins.then_inc(s_pool, 1)
                pool.wait_ge(s_pool, own[0])

            settle(nc.gpsimd.memset(ident[:, :], 0.0))
            nc.gpsimd.affine_select(out=ident[:, :], in_=ident[:, :], compare_op=ALU.not_equal, fill=1.0, base=0,
                                    pattern=[[-1, P]], channel_multiplier=1).then_inc(s_const, 1)
            nc.gpsimd.memset(zero_rows[:, :], 0.0).then_inc(s_const, 1)
            settle(nc.gpsimd.memset(ones_b[:, :], 1.0))
            settle(nc.gpsimd.affine_select(out=tri[:, :], in_=ones_b[:, :], compare_op=ALU.is_gt, fill=0.0, base=0,
                                           pattern=[[1, P]], channel_multiplier=-1))
            nc.gpsimd.iota(iota[:, :], pattern=[[1, P]], base=0, channel_multiplier=0,
                           allow_small_or_imprecise_dtypes=True)
            nc.gpsimd.iota(pcol[:, :], pattern=[[0, 1]], base=0, channel_multiplier=1,
                           allow_small_or_imprecise_dtypes=True)
            nc.gpsimd.iota(vcol[:, :], pattern=[[-P, NT]], base=N, channel_multiplier=-1,
                           allow_small_or_imprecise_dtypes=True).then_inc(s_const, 1)
            settle(nc.gpsimd.memset(m_run[:, :, :], 0.0))
            settle(nc.gpsimd.memset(eq_q[:, :], 1.0))
            settle(nc.gpsimd.affine_select(out=eq_q[:, :], in_=eq_q[:, :], compare_op=ALU.is_ge, fill=0.0, base=0,
                                           pattern=[[-NT, E]], channel_multiplier=1))
            settle(nc.gpsimd.affine_select(out=eq_q[:, :], in_=eq_q[:, :], compare_op=ALU.is_ge, fill=0.0,
                                           base=NT - 1, pattern=[[NT, E]], channel_multiplier=-1)
                   )
            settle(nc.gpsimd.tensor_copy(kq[:, :], pcol[:, :]))
            for e in range(1, E):
                m = nc.gpsimd.tensor_scalar(wt[:, 0:1], pcol[:, :], float(NT * e), float(-NT), ALU.is_ge, ALU.mult)
                settle(m)
                last = nc.gpsimd.tensor_tensor(kq[:, :], kq[:, :], wt[:, 0:1], ALU.add)
                if e < E - 1:
                    settle(last)
            last.then_inc(s_const, 1)

            def split(e, n):
                pool.wait_ge(s_raw[n], 16 * (e + 1))
                nc.gpsimd.tensor_scalar(ew_part(e, n, 0), raw_part(n), 1.0, 0.0, ALU.mult, ALU.add).then_inc(s_whi, 1)
                pool.wait_ge(s_whi, 3 * e + n + 1)
                nc.gpsimd.tensor_tensor(ew_part(e, n, 1), raw_part(n), ew_part(e, n, 0).bitcast(F32),
                                        ALU.subtract).then_inc(s_ew, 1)

            pool.wait_ge(s_lo, S1 + 2 * NT)
            split(0, 0)
            split(0, 1)
            pool.wait_ge(s_lo, S1 + 3 * NT)
            split(0, 2)
            pool.wait_ge(s_lo, 2 * S1)
            for n in range(3):
                split(1, n)

            pool.wait_ge(s_slots, 1)
            pool.wait_ge(s_zero, 32)
            pool.wait_ge(s_xn1st, 16 * NC)
            pool.wait_ge(s_x1st, 16 * NC)
            for j in range(TILES):
                if j >= YR:
                    pool.wait_ge(s_xg[j % YR], 16 * (j // YR))
                nc.gpsimd.indirect_dma_start(
                    out=xg[:, j, :], out_offset=None, in_=table[:, :],
                    in_offset=bass.IndirectOffsetOnAxis(ap=idx[:, j:j + 1], axis=0),
                    bounds_check=N + P - 1).then_inc(s_xg[j % YR], 16)

            def wait_now(which, value):
                pool.wait_ge(which, value)
                pool.sem_inc(s_alone, 1)

            def add_rows(j, u):
                wait_now(s_y, j + 1)
                if not (static(j) and j == 0):
                    wait_now(s_sc, 16 * j)
                nc.gpsimd.indirect_dma_start(
                    out=out[:, :], out_offset=bass.IndirectOffsetOnAxis(ap=idx_st[:, u, :], axis=0),
                    in_=y_st[:, u, :], in_offset=None, bounds_check=N + P - 1,
                    compute_op=ALU.add).then_inc(s_sc, 16)

            for u in range(YR):
                add_rows(u, u)
            pool.wait_ge(s_te, 1)
            total = nc.gpsimd.value_load(te_i[0:1, TILES + 1:TILES + 2], min_val=E, max_val=TILES)
            with nc.gpsimd.Fori(1, TILES // YR) as i:
                for u in range(YR):
                    j = i * YR + u
                    with nc.gpsimd.If(total > j):
                        add_rows(j, u)
            for u in range(YR):
                pool.wait_ge(s_xg[u], 16 * (TILES // YR))
            pool.wait_ge(s_sc, 16 * total)

        @block.scalar
        def _(act):
            def roots(n):
                act.wait_ge(s_var, n)
                nc.scalar.activation(std[:, :], mv[:, :, 1], ACT.Sqrt).then_inc(s_sqrt, 1)

            def x_T(t):
                act.wait_ge(s_xtp, t + 1)
                if t >= 2:
                    act.wait_ge(s_zp, t - 1)
                nc.scalar.copy(xTs[:, t % 2, 0, :, :], x_p[t % 2][:, 0:D].rearrange("p (k n) -> p k n", k=KD)
                               ).then_inc(s_xt, 1)

            def z1_hi(t):
                act.wait_ge(s_zp, t + 1)
                nc.scalar.copy(Z[:, 0, t, :], sm[t % 2][:, 0:D]).then_inc(s_zhi, 1)

            def hi_of_block(s):
                layer, c, jb = s // S1, s % S1 // NT, s % NT
                blk = adj_s[:, CT * c:CT * (c + 1), jb * P:(jb + 1) * P]
                dst = ring[:, s % RING, 0, :].rearrange("p (i n) -> p i n", i=CT)
                if s >= RING:
                    act.wait_ge(s_mm, s - RING + 1)
                if layer == 0:
                    act.wait_ge(s_tp, s + 1)
                    src = tp[s % 2][:, :].rearrange("p (i n) -> p i n", i=CT)
                    nc.scalar.copy(dst, src).then_inc(s_hi, 1)
                    nc.scalar.copy(blk, src).then_inc(s_adjT, 1)
                else:
                    nc.scalar.copy(dst, blk).then_inc(s_hi, 1)

            def hidden1(c, f):
                act.wait_ge(s_mm, NT * (c + 1))
                if c == 0:
                    act.wait_ge(s_zero, 32)
                    act.wait_ge(s_bf, 1)
                else:
                    act.wait_ge(s_z2p, CT * c)
                for out_f in (hTs[:, 0, f, :], hTf[:, 1, f, :]):
                    last = nc.scalar.activation(out_f, acc[c % 2][f][:, :], ACT.Relu, bias=bT[:, 0, f:f + 1])
                last.then_inc(s_h1, 1)

            def hidden2(c):
                act.wait_ge(s_mm, S1 + NT * (c + 1))
                if c >= 2:
                    act.wait_ge(s_up, CT * (c - 1))
                else:
                    act.wait_ge(s_z2p, NT)
                for f in range(KD):
                    last = nc.scalar.activation(hT[:, c % 2, f, :], acc[c % 2][f][:, :], ACT.Relu,
                                                bias=bT[:, 1, f:f + 1])
                last.then_inc(s_h2, 1)

            def z_hi(t):
                act.wait_ge(s_z2, t + 1)
                act.wait_ge(s_mm, S1 - NT + t + 1)
                nc.scalar.copy(Z[:, 0, t, :], z2[:, t, :]).then_inc(s_zhi, 1)

            def token_work(c, k):
                if k in (3, 4):
                    for i in (2 * k - 6, 2 * k - 5):
                        act.wait_ge(s_up, CT * c + i + 1)
                        if c >= 1:
                            act.wait_ge(s_x1st, 16 * c)
                        nc.scalar.activation(x1[:, i, :], token_bank(c, i)[:, 0:D], ACT.Tanh).then_inc(s_th, 1)
                if k == 7:
                    roots(NC + c + 1)
                if k in (10, 11):
                    for i in (2 * k - 20, 2 * k - 19):
                        act.wait_ge(s_xtp, NT + CT * c + i + 1)
                        nc.scalar.copy(xT[:, i, :, :],
                                       token_bank(c, i)[:, 0:D].rearrange("p (k n) -> p k n", k=KD)).then_inc(s_xt, 1)
                if k == NT:
                    act.wait_ge(s_dlt, c + 1)
                    nc.scalar.activation(ex[:, :], dlt[:, :], ACT.Exp).then_inc(s_exp, 1)
                for n in range(2 * CT):
                    if k == HOT[c][n] + 1:
                        _, mask, s3, _ = oh_slot(c, n)
                        act.wait_ge(s_mask, 2 * CT * c + n + 1)
                        for a in range(2):
                            last = nc.scalar.activation(s3[:, (a + 1) * P:(a + 2) * P], mask, ACT.Copy,
                                                        scale=whi2[:, c % 2, a, n:n + 1].bitcast(F32))
                        last.then_inc(s_ohw, 1)

            roots(1)
            x_T(0)
            x_T(1)
            z1_hi(0)
            for s in range(2 * S1):
                layer, c, jb = s // S1, s % S1 // NT, s % NT
                if s == S1:
                    act.wait_ge(s_adjT, S1)
                hi_of_block(s)
                if s < NT - CT and s % CT == 1:
                    roots(2 + s // CT)
                if s == CT:
                    act.wait_ge(s_const, 2)
                    for rows in (table, out):
                        act.dma_start(rows[N:N + P, :], zero_rows[:, :]).then_inc(s_zero, 16)
                if s < NT - 1:
                    if s < NT - 2:
                        x_T(s + 2)
                    z1_hi(s + 1)
                if NT <= s < S1 + NT and jb in (1, 2):
                    hidden1(s // NT - 1, jb - 1)
                if jb == 1 and s > S1 + NT:
                    hidden2(c - 1)
                if layer == 0 and c == NC - 1 and 2 <= jb < NT - CT + 2:
                    z_hi(jb - 2)
                if layer == 1 and c == 0 and 7 <= jb < 7 + CT:
                    z_hi(NT - CT + jb - 7)
                if layer == 1 and c >= 2:
                    token_work(c - 2, NT + jb)
                if layer == 1 and c >= 1:
                    token_work(c - 1, jb)
            hidden2(NC - 1)
            for k in range(STEPS):
                token_work(NC - 2, NT + k)
                token_work(NC - 1, k)
            act.wait_ge(s_exp, NC)
            nc.scalar.activation(dlt[:, :], ex[:, :], ACT.Silu).then_inc(s_alone, 1)

            def xe_hi(j):
                act.wait_ge(s_xep, j + 1)
                if not (static(j) and j == 0):
                    act.wait_ge(s_ab, 2 * j)
                nc.scalar.copy(xeT[:, 0, :, :], xe_p[:, 0:D].rearrange("p (k n) -> p k n", k=KD)).then_inc(s_xehi, 1)

            def y_out(j, u):
                act.wait_ge(s_yp, j + 1)
                if not static(j) or j >= YR:
                    act.wait_ge(s_sc, 16 * (j - YR + 1))
                nc.scalar.copy(idx_st[:, u, :], idx[:, bass.ds(j, 1)])
                nc.scalar.activation(y_st[:, u, :], y_p[:, 0:D], ACT.Copy,
                                     scale=wt[:, bass.ds(j, 1)]).then_inc(s_y, 1)

            def third_hi(e, buf, n):
                act.wait_ge(s_raw[n], 16 * (e + 1))
                nc.scalar.copy(ew_part(buf, n, 0), raw_part(n)).then_inc(s_whi, 1)

            def tile(j, u, plan=None):
                for h in range(2):
                    if plan:
                        refill(nc.scalar, plan, h, third_hi)
                    act.wait_ge(s_ab, 2 * j + h + 1)
                    if not (static(j) and j == 0):
                        act.wait_ge(s_he, 2 * j + h - 1)
                    nc.scalar.activation(sil[:, h, :], up_p[h][:, :], ACT.Silu).then_inc(s_sil, 1)
                if not (static(j) and j == TILES - 1):
                    xe_hi(j + 1)
                if not (static(j) and j == 0):
                    y_out(j - 1, (u - 1) % YR)
                for h in range(2):
                    act.wait_ge(s_hep, 2 * j + h + 1)
                    nc.scalar.copy(heT[:, 0, CT * h:CT * (h + 1), :],
                                   heT_p[h][:, :].rearrange("p (k n) -> p k n", k=CT)).then_inc(s_hehi, 1)

            def guarded(j, u):
                with nc.scalar.If(total > j):
                    plan = plan_of(nc.scalar, j)
                    tile(j, u, plan)
                    refill(nc.scalar, plan, 2, third_hi)
                    act.sem_inc(s_alone, 1)
                with nc.scalar.If(total == j):
                    y_out(j - 1, (u - 1) % YR)

            xe_hi(0)
            act.wait_ge(s_te, 1)
            tile(0, 0)
            act.wait_ge(s_ew, 6)
            for u in range(1, YR):
                plan = plan_of(nc.scalar, u)
                tile(u, u, plan)
                refill(nc.scalar, plan, 2, third_hi)
            total = nc.scalar.value_load(te_i[0:1, TILES + 1:TILES + 2], min_val=E, max_val=TILES)
            with act.Fori(1, TILES // YR) as i:
                for u in range(YR):
                    guarded(i * YR + u, u)
            with nc.scalar.If(total == TILES):
                y_out(TILES - 1, YR - 1)

        @block.vector
        def _(dve):
            own = [0]

            def settle(ins):
                own[0] += 1
                ins.then_inc(s_dve, 1)
                dve.wait_ge(s_dve, own[0])

            def stats_of(src, tiles):
                for i in tiles:
                    last = nc.vector.bn_stats(stats[:, i, :], src(i))
                settle(last)

            def spread():
                for i in range(CT):
                    last = nc.vector.bn_aggr(mv[:, i, :], stats[:, i, :])
                settle(last)
                nc.vector.tensor_scalar(mv[:, :, 1], mv[:, :, 1], EPS, None, ALU.add).then_inc(s_var, 1)

            def roots(n):
                dve.wait_ge(s_sqrt, n)
                settle(nc.vector.reciprocal(rstd[:, :], std[:, :]))

            def x_norm(g, part):
                if part < 2:
                    dve.wait_ge(s_x[g], 16)
                    stats_of(lambda i: x_in[:, CT * g + i, :], (2 * part, 2 * part + 1))
                if part == 1:
                    spread()
                if part == 2:
                    roots(g + 1)
                    for i in range(CT):
                        v = x_in[:, CT * g + i, :]
                        last = nc.vector.tensor_scalar(v, v, mv[:, i, 0:1], rstd[:, i:i + 1],
                                                       ALU.subtract, ALU.mult)
                    last.then_inc(s_xn, 1)

            def x_T_lo(t):
                dve.wait_ge(s_xt, t + 1)
                nc.vector.tensor_tensor(xTs[:, t % 2, 1, :, :], x_p[t % 2][:, 0:D].rearrange("p (k n) -> p k n", k=KD),
                                        xTs[:, t % 2, 0, :, :].bitcast(F32), ALU.subtract).then_inc(s_xtlo, 1)

            def z1_lo(t):
                dve.wait_ge(s_zhi, t + 1)
                nc.vector.tensor_tensor(Z[:, 1, t, :], sm[t % 2][:, 0:D], Z[:, 0, t, :].bitcast(F32),
                                        ALU.subtract).then_inc(s_zlo, 1)

            def lo_of_block(s):
                layer, c, jb = s // S1, s % S1 // NT, s % NT
                if layer == 0:
                    dve.wait_ge(s_adjT, s + 1)
                else:
                    dve.wait_ge(s_hi, s + 1)
                hi = ring[:, s % RING, 0, :].bitcast(F32).rearrange("p (i n) -> p i n", i=CT)
                lo = ring[:, s % RING, 1, :].rearrange("p (i n) -> p i n", i=CT)
                src = adj_s[:, CT * c:CT * (c + 1), jb * P:(jb + 1) * P]
                nc.vector.tensor_tensor(lo, src, hi, ALU.subtract).then_inc(s_lo, 1)

            def z_lo(t):
                dve.wait_ge(s_zhi, NT + t + 1)
                nc.vector.tensor_tensor(Z[:, 1, t, :], z2[:, t, :], Z[:, 0, t, :].bitcast(F32),
                                        ALU.subtract).then_inc(s_zlo, 1)

            def h_lo(c):
                dve.wait_ge(s_h1, KD * (c + 1))
                nc.vector.tensor_tensor(hTs[:, 1, :, :], hTf[:, 1, :, :], hTs[:, 0, :, :].bitcast(F32),
                                        ALU.subtract).then_inc(s_hlo, 1)

            def z2_out(t):
                dve.wait_ge(s_z2p, t + 1)
                nc.vector.tensor_copy(z2[:, t, :], sm[t % 2][:, 0:D]).then_inc(s_z2, 1)

            def bc(v, n):
                return v.unsqueeze(len(v.shape)).to_broadcast(list(v.shape) + [n])

            def mark(ins):
                own[0] += 1
                return ins.then_inc(s_dve, 1)

            def marked():
                dve.wait_ge(s_dve, own[0])

            def tile_counts(n):
                tq = tmp_j[:, 0:2 * E].rearrange("p (a e) -> p a e", a=2)
                if n == 0:
                    dve.wait_ge(s_cnt, 1)
                    mark(nc.vector.tensor_scalar(cnt_i[:, :], cnt_p, float(P - 1), None, ALU.add))
                    mark(nc.vector.memset(end[:, :], 1.0))
                if n == 1:
                    marked()
                    mark(nc.vector.tensor_scalar(cnt_i[:, :], cnt_i[:, :], P.bit_length() - 1, None,
                                                 ALU.logical_shift_right))
                if n == 2:
                    marked()
                    settle(nc.vector.tensor_copy(cnt[:, :], cnt_i[:, :]))
                    mark(nc.vector.tensor_scalar(tl[:, 1, :], cnt[:, :], 1.0, None, ALU.max))
                if n == 3:
                    marked()
                    settle(nc.vector.tensor_tensor_scan(cnt[:, :], end[:, :], tl[:, 1, :], 0.0, ALU.mult, ALU.add))
                    mark(nc.vector.tensor_copy(end[:, :], cnt[:, :]))
                if n == 4:
                    marked()
                    settle(nc.vector.tensor_tensor(tl[:, 0, :], end[:, :], tl[:, 1, :], ALU.subtract))
                    for a in range(2):
                        mark(nc.vector.tensor_tensor(tq[:, a, :], tl[:, a, :], eq_q[:, :], ALU.mult))
                if n == 5:
                    marked()
                    mark(nc.vector.tensor_reduce(sq[:, :], tq, AX.X, ALU.add))
                if n == 6:
                    marked()
                    mark(nc.vector.tensor_scalar(sq[:, 0:1], sq[:, 0:1], kq[:, :], 1.0, ALU.add, ALU.add))
                    mark(nc.vector.tensor_tensor(sq[:, 1:2], kq[:, :], sq[:, 1:2], ALU.is_lt))
                if n == 7:
                    marked()
                    settle(nc.vector.tensor_scalar(sq[:, 0:1], sq[:, 0:1], sq[:, 1:2], -1.0, ALU.mult, ALU.add))
                    settle(nc.vector.tensor_scalar(sel[:, 0:TILES], iota[:, 0:TILES], sq[:, 0:1], None,
                                                   ALU.is_equal))

            def one_hot(c, n):
                m = 2 * CT * c + n
                t = CT * c + n % CT
                if n == 0:
                    dve.wait_ge(s_qs, c + 1)
                q, mask, s3, mapped = oh_slot(c, n)
                if c == NC - 2 and n in (2, 3):
                    dve.wait_ge(s_mm, 2 * S1)
                elif mapped > 0:
                    dve.wait_ge(s_inf, mapped)
                nc.vector.tensor_scalar(q, iota[:, :], qf[:, n:n + 1], None, ALU.is_equal)
                nc.vector.tensor_scalar(mask, iota[:, :], sf[:, n:n + 1], None, ALU.is_equal).then_inc(s_mask, 1)
                nc.vector.tensor_scalar(s3[:, 0:P], iota[:, :], sf[:, n:n + 1], vcol[:, t:t + 1],
                                        ALU.is_equal, ALU.mult).then_inc(s_oh, 1)
                if c == NC - 1:
                    tile_counts(n)

            def token_work(c, k):
                tiles = {4: (0, 1), 5: (2,), 6: (3,)}.get(k, ())
                for i in tiles:
                    dve.wait_ge(s_th, CT * c + i + 1)
                    dve.wait_ge(s_xres, 16 * (c + 1))
                    nc.vector.tensor_tensor(x1[:, i, :], x1[:, i, :], x_res[:, i, :], ALU.add).then_inc(s_x1, 1)
                for i in tiles:
                    dve.wait_ge(s_x1, CT * c + i + 1)
                    mark(nc.vector.bn_stats(stats[:, i, :], x1[:, i, :]))
                if k == 6:
                    marked()
                    spread()
                if k == 8:
                    roots(NC + c + 1)
                if k in (8, 9):
                    for i in (2 * k - 16, 2 * k - 15):
                        nc.vector.tensor_scalar(xn1[:, i, :], x1[:, i, :], mv[:, i, 0:1], rstd[:, i:i + 1],
                                                ALU.subtract, ALU.mult).then_inc(s_xn1, 1)
                if k == NT - 2:
                    dve.wait_ge(s_gate, CT * (c + 1))
                    g = gate_p.rearrange("p (i e) -> p i e", e=E)
                    for i in range(CT):
                        last = nc.vector.max(out=m8[:, i, :], in_=g[:, i, :])
                    settle(last)
                    for i in range(CT):
                        last = nc.vector.max_index(out=ix8[:, i, :], in_max=m8[:, i, :], in_values=g[:, i, :])
                    settle(last)
                    nc.vector.tensor_tensor(dlt[:, :], m8[:, :, 1], m8[:, :, 0], ALU.subtract).then_inc(s_dlt, 1)
                    nc.vector.tensor_copy(idxf[:, :, :], ix8[:, :, 0:2].rearrange("p i k -> p k i")).then_inc(s_idxf, 1)
                if k == NT - 1:
                    dve.wait_ge(s_idxf, c + 1)
                    io = iota[:, 0:E].unsqueeze(1).to_broadcast([P, 2 * CT, E])
                    ohv = oh[:, :, :, :].rearrange("p k i e -> p (k i) e")
                    settle(nc.vector.tensor_tensor(ohv, io, bc(idxf.rearrange("p k i -> p (k i)"), E), ALU.is_equal))
                    if c >= 1:
                        settle(nc.vector.tensor_copy(m_run[:, 0, :], m_run[:, CT, :]))
                    mb = m_bf[:, 0, :].rearrange("p (i e) -> p i e", e=E)
                    settle(nc.vector.tensor_tensor(mb, oh[:, 0, :, :], oh[:, 1, :, :], ALU.add))
                    for i in range(CT):
                        settle(nc.vector.tensor_tensor(m_run[:, i + 1, :], m_run[:, i, :], mb[:, i, :], ALU.add))
                    nc.vector.tensor_copy(m_bf[:, 2, 0:E], m_run[:, CT, :])
                    nc.vector.tensor_copy(m_bf[:, 1, :].rearrange("p (i e) -> p i e", e=E),
                                          m_run[:, 0:CT, :]).then_inc(s_m, 1)
                if k == SLOTS[c]:
                    dve.wait_ge(s_pos, c + 1)
                    for k2 in range(2):
                        last = nc.vector.tensor_tensor(ohpos[:, k2, :, :], oh[:, k2, :, :],
                                                       pos_p.rearrange("p (i e) -> p i e", e=E), ALU.mult)
                    settle(last)
                    settle(nc.vector.tensor_reduce(posk[:, :, :], ohpos[:, :, :, :], AX.X, ALU.add))
                    dve.wait_ge(s_exp, c + 1)
                    nc.vector.tensor_scalar(wk[:, 1, :], ex[:, :], 1.0, None, ALU.add)
                    settle(nc.vector.scalar_tensor_tensor(
                        out=gsl[:, :], in0=idxf.rearrange("p k i -> p (k i)"), scalar=float(N),
                        in1=posk.rearrange("p k i -> p (k i)"), op0=ALU.mult, op1=ALU.add))
                    shift = P.bit_length() - 1
                    nc.vector.reciprocal(wk[:, 0, :], wk[:, 1, :])
                    nc.vector.tensor_scalar(qi[:, :], gsl[:, :], shift, None, ALU.logical_shift_right)
                    settle(nc.vector.tensor_scalar(si[:, :], gsl[:, :], P - 1, None, ALU.bitwise_and))
                    nc.vector.tensor_tensor(wk[:, 1, :], ex[:, :], wk[:, 0, :], ALU.mult)
                    nc.vector.tensor_copy(qf[:, :], qi[:, :])
                    settle(nc.vector.tensor_copy(sf[:, :], si[:, :]))
                    wkf = wk.rearrange("p k i -> p (k i)")
                    whi = whi2[:, c % 2, :, :]
                    settle(nc.vector.tensor_copy(whi[:, 0, :], wkf))
                    nc.vector.tensor_tensor(whi[:, 1, :], wkf, whi[:, 0, :].bitcast(F32),
                                            ALU.subtract).then_inc(s_qs, 1)
                for n in range(2 * CT):
                    if k == HOT[c][n]:
                        one_hot(c, n)

            def split_bf():
                dve.wait_ge(s_w, 7 * 16)
                sign = bf_sign[:, :]
                nc.vector.tensor_scalar(one_rows[:, :], iota[0:2, :], 0.0, 1.0, ALU.mult, ALU.add)
                nc.vector.tensor_scalar(sign, pcol[0:2, :], -2.0, 1.0, ALU.mult, ALU.add)
                settle(nc.vector.tensor_copy(bf_hi[:, :], bf_in[:, :]))
                settle(nc.vector.tensor_scalar(bf_hi[:, :], bf_hi[:, :].bitcast(F32), sign, None, ALU.mult))
                nc.vector.scalar_tensor_tensor(out=bf_parts[:, :], in0=bf_in[:, :], scalar=pcol[0:2, :],
                                               in1=bf_hi[:, :].bitcast(F32), op0=ALU.mult, op1=ALU.add).then_inc(s_bf, 1)

            dve.wait_ge(s_const, 3)
            for part in range(3):
                x_norm(0, part)
                if part == 0:
                    dve.wait_ge(s_w1, 16)
                    settle(nc.vector.tensor_copy(W1s[:, 0, :, :], Wg[:, 0, :, :]))
                    nc.vector.tensor_tensor(W1s[:, 1, :, :], Wg[:, 0, :, :], W1s[:, 0, :, :].bitcast(F32),
                                            ALU.subtract).then_inc(s_w1s, 1)
            x_T_lo(0)
            x_T_lo(1)
            x_norm(1, 0)
            z1_lo(0)
            for s in range(2 * S1):
                layer, c, jb = s // S1, s % S1 // NT, s % NT
                if s == S1:
                    dve.wait_ge(s_adjT, S1)
                lo_of_block(s)
                if s < NT - CT - 1 and (s + 1) % CT < 3:
                    x_norm(1 + (s + 1) // CT, (s + 1) % CT)
                if s < NT - 2:
                    x_T_lo(s + 2)
                if s < NT - 1:
                    z1_lo(s + 1)
                if s == NT - 5:
                    dve.wait_ge(s_const, 4)
                    split_bf()
                if s == NT - 3:
                    settle(nc.vector.tensor_copy(W3s[:, 0, :, :], Wg[:, 1, :, :]))
                    nc.vector.tensor_tensor(W3s[:, 1, :, :], Wg[:, 1, :, :], W3s[:, 0, :, :].bitcast(F32),
                                            ALU.subtract).then_inc(s_w3s, 1)
                if NT <= s < S1 + NT:
                    before = s // NT - 1
                    if jb == 3:
                        h_lo(before)
                    if jb in (5, 6):
                        z2_out(CT * before + 2 * jb - 10)
                        z2_out(CT * before + 2 * jb - 9)
                if layer == 0 and c == NC - 1 and 2 <= jb < NT - CT + 2:
                    z_lo(jb - 2)
                if layer == 1 and c == 0 and 7 <= jb < 7 + CT:
                    z_lo(NT - CT + jb - 7)
                if layer == 1 and c >= 2:
                    token_work(c - 2, NT + jb)
                if layer == 1 and c >= 1:
                    token_work(c - 1, jb)
            for k in range(STEPS):
                token_work(NC - 2, NT + k)
                token_work(NC - 1, k)

            dve.wait_ge(s_inf, 2 * NT)
            nc.vector.tensor_copy(info[:, 0, :], info_p[:, 0:P]).then_inc(s_sel, 1)
            settle(nc.vector.tensor_copy(info[:, 1, :], info_p[:, P:2 * P]))
            nc.vector.tensor_tensor(info[:, 1, :], info[:, 1, :], info_p[:, 2 * P:3 * P], ALU.add).then_inc(s_sel, 1)
            dve.wait_ge(s_selp, 1)
            pad = tmp_j[:, 640:640 + TILES]
            settle(nc.vector.tensor_scalar(pad, sel_p, 0.0, pcol[:, :], ALU.is_equal, ALU.mult))
            nc.vector.scalar_tensor_tensor(out=idx[:, :], in0=pad, scalar=float(N), in1=sel_p,
                                           op0=ALU.add, op1=ALU.subtract).then_inc(s_slots, 1)
            dve.wait_ge(s_selp, 2)
            nc.vector.tensor_copy(wt[:, :], wt_p)
            TU = TILES + 1
            cmp = tmp_j[0:1, 16:16 + TU * (E - 1)].rearrange("p (j e) -> p j e", e=E - 1)
            te, use, fill, wk_t = (tmp_j[0:1, 700 + TU * a:700 + TU * (a + 1)] for a in range(4))
            ej = end[0:1, 0:E - 1].unsqueeze(1).to_broadcast([1, TU, E - 1])
            settle(nc.vector.tensor_tensor(cmp, ej, bc(iota[0:1, 0:TU], E - 1), ALU.is_le))
            nc.vector.tensor_scalar(use, iota[0:1, 0:TU], end[0:1, E - 1:E], None, ALU.is_lt)
            nc.vector.tensor_scalar(wk_t, iota[0:1, 0:TU], end[0:1, E - 1:E], 2.0, ALU.is_equal, ALU.mult)
            settle(nc.vector.tensor_reduce(te, cmp, AX.X, ALU.add))
            nc.vector.tensor_tensor(use, use, wk_t, ALU.add)
            nc.vector.memset(fill[:, 0:1], 0.0)
            settle(nc.vector.tensor_scalar(te_i[:, 0:TU], te, 1.0, None, ALU.add))
            nc.vector.tensor_tensor(fill[:, 1:TU], te[:, 1:TU], te[:, 0:TU - 1], ALU.subtract)
            nc.vector.tensor_scalar(wk_t, te, float(E - 2), None, ALU.is_le)
            settle(nc.vector.tensor_scalar(te_i[:, 0:TU], te_i[:, 0:TU], 1, None, ALU.bitwise_and))
            settle(nc.vector.tensor_tensor(fill, fill, wk_t, ALU.mult))
            settle(nc.vector.tensor_copy(wk_t, te_i[:, 0:TU]))
            settle(nc.vector.scalar_tensor_tensor(out=fill, in0=wk_t, scalar=1.0, in1=fill,
                                                  op0=ALU.add, op1=ALU.mult))
            settle(nc.vector.scalar_tensor_tensor(out=fill, in0=fill, scalar=4.0, in1=use,
                                                  op0=ALU.mult, op1=ALU.add))
            settle(nc.vector.tensor_scalar(fill, fill, float(E), None, ALU.mult))
            settle(nc.vector.tensor_tensor(fill[:, 1:TU], fill[:, 1:TU], te[:, 0:TU - 1], ALU.add))
            settle(nc.vector.scalar_tensor_tensor(out=te_i[:, 0:TU], in0=fill, scalar=float(E), in1=te,
                                                  op0=ALU.mult, op1=ALU.add))
            nc.vector.tensor_copy(te_i[:, TU:TU + 1], end[0:1, E - 1:E]).then_inc(s_te, 1)

            def row_copy(j, u, i):
                dve.wait_ge(s_xg[u], 16 * (i + 1))
                if not (static(j) and j == 0):
                    dve.wait_ge(s_xep, j)
                nc.vector.tensor_copy(xs[:, :], xg[:, bass.ds(j, 1), :].rearrange("p o d -> p (o d)")).then_inc(s_xs, 1)

            def xe_lo(j):
                dve.wait_ge(s_xehi, j + 1)
                nc.vector.tensor_tensor(xeT[:, 1, :, :], xe_p[:, 0:D].rearrange("p (k n) -> p k n", k=KD),
                                        xeT[:, 0, :, :].bitcast(F32), ALU.subtract).then_inc(s_xelo, 1)

            def third_lo(e, buf, n):
                dve.wait_ge(s_whi, 3 * e + n + 1)
                nc.vector.tensor_tensor(ew_part(buf, n, 1), raw_part(n), ew_part(buf, n, 0).bitcast(F32),
                                        ALU.subtract).then_inc(s_ew, 1)

            def tile(j, u, i, plan=None):
                if not (static(j) and j == TILES - 1):
                    row_copy(j + 1, (u + 1) % YR, i + (u + 1) // YR)
                if plan:
                    refill(nc.vector, plan, 0, third_lo)
                for h in range(2):
                    dve.wait_ge(s_sil, 2 * j + h + 1)
                    if not (static(j) and j == 0):
                        dve.wait_ge(s_hep, 2 * j)
                    nc.vector.tensor_tensor(he[:, h * HW:(h + 1) * HW], sil[:, h, :], up_p[2 + h][:, :],
                                            ALU.mult).then_inc(s_he, 1)
                if not (static(j) and j == TILES - 1):
                    xe_lo(j + 1)
                if plan:
                    refill(nc.vector, plan, 1, third_lo)
                for h in range(2):
                    dve.wait_ge(s_hehi, 2 * j + h + 1)
                    nc.vector.tensor_tensor(heT[:, 1, CT * h:CT * (h + 1), :],
                                            heT_p[h][:, :].rearrange("p (k n) -> p k n", k=CT),
                                            heT[:, 0, CT * h:CT * (h + 1), :].bitcast(F32),
                                            ALU.subtract).then_inc(s_helo, 1)

            def guarded(j, u, i):
                with nc.vector.If(total > j):
                    plan = plan_of(nc.vector, j)
                    tile(j, u, i, plan)
                    refill(nc.vector, plan, 2, third_lo)
                    dve.sem_inc(s_alone, 1)

            dve.wait_ge(s_te, 1)
            row_copy(0, 0, 0)
            xe_lo(0)
            tile(0, 0, 0)
            dve.wait_ge(s_ew, 6)
            for u in range(1, YR):
                plan = plan_of(nc.vector, u)
                tile(u, u, 0, plan)
                refill(nc.vector, plan, 2, third_lo)
            total = nc.vector.value_load(te_i[0:1, TILES + 1:TILES + 2], min_val=E, max_val=TILES)
            with dve.Fori(1, TILES // YR - 1) as i:
                for u in range(YR):
                    guarded(i * YR + u, u, i)
            for u in range(YR):
                guarded(TILES - YR + u, u, TILES // YR - 1)

        @block.tensor
        def _(pe):
            pe.wait_ge(s_const, 3)
            pe.wait_ge(s_w1, 16)

            def x_T(t):
                pe.wait_ge(s_xn, t // CT + 1)
                if t >= 2:
                    pe.wait_ge(s_xtlo, t - 1)
                for k in range(KD):
                    last = nc.tensor.transpose(x_p[t % 2][:, k * P:(k + 1) * P], x_in[:, t, k * P:(k + 1) * P],
                                               ident[:, :])
                last.then_inc(s_xtp, 1)

            def z1_rows(t):
                pe.wait_ge(s_w1s, 1)
                pe.wait_ge(s_xtlo, t + 1)
                if t >= 2:
                    pe.wait_ge(s_zlo, t - 1)
                for k in range(KD):
                    for xl, wl in ((0, 0), (0, 1), (1, 0)):
                        last = nc.tensor.matmul(sm[t % 2][:, 0:D], xTs[:, t % 2, xl, k, :], W1s[:, wl, k, :],
                                                start=(k == xl == wl == 0), stop=(k == KD - 1 and xl == 1))
                last.then_inc(s_zp, 1)

            def transpose_block(s):
                c, jb = s // NT, s % NT
                if jb == 0:
                    for par in range(2):
                        pe.wait_ge(s_adj[par], 16 * (CT * (c + 1) // 2))
                if s >= 2:
                    pe.wait_ge(s_adjT, s - 1)
                for i in range(CT):
                    last = nc.tensor.transpose(tp[s % 2][:, i * P:(i + 1) * P],
                                               adj_s[:, CT * c + i, jb * P:(jb + 1) * P], ident[:, :])
                last.then_inc(s_tp, 1)

            def product(s):
                n, jb = s // NT, s % NT
                pe.wait_ge(s_lo, s + 1)
                if n == 0:
                    pe.wait_ge(s_zlo, jb + 1)
                if n == NC:
                    pe.wait_ge(s_zlo, NT + jb + 1)
                if jb == 0 and n >= 2:
                    if n - 2 < NC:
                        pe.wait_ge(s_h1, KD * (n - 1))
                    else:
                        pe.wait_ge(s_h2, n - 1 - NC)
                    if n >= NC + 2:
                        pe.wait_ge(s_xt, NT + CT * (n - NC - 1))
                hi, lo = ring[:, s % RING, 0, :], ring[:, s % RING, 1, :]
                for f in range(KD):
                    zh = Z[:, 0, jb, f * P:(f + 1) * P]
                    zl = Z[:, 1, jb, f * P:(f + 1) * P]
                    a = acc[n % 2][f][:, :]
                    nc.tensor.matmul(a, zh, hi, start=(jb == 0), stop=False)
                    nc.tensor.matmul(a, zh, lo, start=False, stop=False)
                    last = nc.tensor.matmul(a, zl, hi, start=False, stop=(jb == NT - 1))
                last.then_inc(s_mm, 1)

            def z2_rows(t):
                c = t // CT
                pe.wait_ge(s_w3s, 1)
                pe.wait_ge(s_hlo, c + 1)
                if t >= 2:
                    pe.wait_ge(s_z2, t - 1)
                for k in range(KD):
                    for hl, wl in ((0, 0), (0, 1), (1, 0)):
                        last = nc.tensor.matmul(sm[t % 2][:, 0:D], hTs[:, hl, k, (t % CT) * P:(t % CT + 1) * P],
                                                W3s[:, wl, k, :], start=(k == hl == wl == 0),
                                                stop=(k == KD - 1 and hl == 1))
                last.then_inc(s_z2p, 1)

            def slot_map(c, n):
                m = 2 * CT * c + n
                pe.wait_ge(s_oh, m + 1)
                pe.wait_ge(s_ohw, m + 1)
                q, _, s3, _ = oh_slot(c, n)
                nc.tensor.matmul(info_p[:, 0:3 * P], q, s3, start=(m == 0),
                                 stop=(m == 2 * NT - 1)).then_inc(s_inf, 1)

            def token_work(c, k):
                if k in (2, 3):
                    for i in (2 * k - 4, 2 * k - 3):
                        b = token_bank(c, i)[:, 0:D]
                        pe.wait_ge(s_h2, c + 1)
                        if c == 0:
                            pe.wait_ge(s_z2, NT)
                            pe.wait_ge(s_bf, 1)
                        nc.tensor.matmul(b, one_rows[:, :], bf_parts[:, :], start=True, stop=False)
                        for f in range(KD):
                            last = nc.tensor.matmul(b, hT[:, c % 2, f, i * P:(i + 1) * P], Wg[:, 2, f, :],
                                                    start=False, stop=(f == KD - 1))
                        last.then_inc(s_up, 1)
                if k in (9, 10):
                    for i in (2 * k - 18, 2 * k - 17):
                        pe.wait_ge(s_xn1, CT * c + i + 1)
                        for f in range(KD):
                            last = nc.tensor.transpose(token_bank(c, i)[:, f * P:(f + 1) * P],
                                                       xn1[:, i, f * P:(f + 1) * P], ident[:, :])
                        last.then_inc(s_xtp, 1)
                if k in (11, 12):
                    for i in (2 * k - 22, 2 * k - 21):
                        pe.wait_ge(s_xt, NT + CT * c + i + 1)
                        if c >= 1:
                            pe.wait_ge(s_qs, c)
                        for f in range(KD):
                            last = nc.tensor.matmul(gate_p[:, i * E:(i + 1) * E], xT[:, i, f, :], gw[:, f, :],
                                                    start=(f == 0), stop=(f == KD - 1))
                        last.then_inc(s_gate, 1)
                if k == NT:
                    pe.wait_ge(s_m, c + 1)
                    nc.tensor.matmul(pos_p, tri[:, :], m_bf[:, 0, :], start=True, stop=False)
                    nc.tensor.matmul(pos_p, ones_b[:, :], m_bf[:, 1, :], start=False, stop=True).then_inc(s_pos, 1)
                for n in range(2 * CT):
                    if k == HOT[c][n] + 1:
                        slot_map(c, n)

            for t in range(2):
                x_T(t)
            z1_rows(0)
            transpose_block(0)
            transpose_block(1)
            for s in range(2 * S1):
                layer, c, jb = s // S1, s % S1 // NT, s % NT
                if s == NT:
                    pe.wait_ge(s_w, 7 * 16)
                if s < NT - 1:
                    if s < NT - 2:
                        x_T(s + 2)
                    z1_rows(s + 1)
                if s + 2 < S1:
                    transpose_block(s + 2)
                product(s)
                if NT <= s < S1 + NT and jb in (4, 5):
                    z2_rows(CT * (s // NT - 1) + 2 * jb - 8)
                    z2_rows(CT * (s // NT - 1) + 2 * jb - 7)
                if layer == 1 and c >= 2:
                    token_work(c - 2, NT + jb)
                if layer == 1 and c >= 1:
                    token_work(c - 1, jb)
            for k in range(NT + 1):
                token_work(NC - 2, NT + k)
                token_work(NC - 1, k)
            nc.tensor.matmul(cnt_p, ones_b[:, :], m_bf[:, 2, 0:E], start=True, stop=True).then_inc(s_cnt, 1)
            for k in range(NT + 1, STEPS):
                token_work(NC - 2, NT + k)
                token_work(NC - 1, k)
            for a, b in enumerate((sel_p, wt_p)):
                pe.wait_ge(s_sel, a + 1)
                nc.tensor.matmul(b, info[:, a, :], sel[:, 0:TILES], start=True, stop=True).then_inc(s_selp, 1)

            def rows_T(j):
                pe.wait_ge(s_xs, j + 1)
                if not (static(j) and j == 0):
                    pe.wait_ge(s_xelo, j)
                for k in range(KD):
                    last = nc.tensor.transpose(xe_p[:, k * P:(k + 1) * P], xs[:, k * P:(k + 1) * P], ident[:, :])
                last.then_inc(s_xep, 1)

            def three(out_ap, k0, k1, stat, w_at):
                for k in range(k0, k1):
                    for sl, wl in ((0, 0), (0, 1), (1, 0)):
                        last = nc.tensor.matmul(out_ap, stat[:, sl, k, :], w_at(k, wl),
                                                start=(k == k0 and sl == wl == 0), stop=(k == k1 - 1 and sl == 1))
                return last

            def up_from(j, buf):
                for h in range(2):
                    if not (static(j) and j == 0):
                        pe.wait_ge(s_he, 2 * j - 1 + h)
                    for m in range(2):
                        o = buf * EWS + m * H + h * HW
                        last = three(up_p[2 * m + h][:, :], 0, KD, xeT,
                                     lambda k, lo: ew[:, o + 4 * H * lo + 2 * H * k:][:, 0:HW])
                    last.then_inc(s_ab, 1)

            def down_from(buf):
                o = buf * EWS + 8 * H
                three(y_p[:, 0:D], 0, KH, heT, lambda k, lo: ew[:, o + 2 * H * lo + D * k:][:, 0:D]).then_inc(s_yp, 1)

            def up(j, e):
                pe.wait_ge(s_ew, 3 * e + 2)
                pe.wait_ge(s_xelo, j + 1)
                side = e % 2
                for buf in range(2):
                    with nc.tensor.If(side == buf):
                        up_from(j, buf)

            def down(j, e):
                pe.wait_ge(s_ew, 3 * e + 3)
                pe.wait_ge(s_helo, 2 * j + 2)
                if not (static(j) and j == 0):
                    pe.wait_ge(s_y, j)
                if static(e):
                    down_from(e % 2)
                    return
                side = e % 2
                for buf in range(2):
                    with nc.tensor.If(side == buf):
                        down_from(buf)

            def hidden_T(j):
                for h in range(2):
                    pe.wait_ge(s_he, 2 * j + h + 1)
                    for k in range(CT):
                        last = nc.tensor.transpose(heT_p[h][:, k * P:(k + 1) * P],
                                                   he[:, (CT * h + k) * P:(CT * h + k + 1) * P], ident[:, :])
                    last.then_inc(s_hep, 1)

            def outputs_before(j, plan):
                with nc.tensor.If(plan[2] > 0):
                    down(j - 1, plan[1])

            def middle(j, plan, last=False):
                outputs_before(j, plan)
                following = plan_of(nc.tensor, j + 1)
                with nc.tensor.If(plan[2] == 1):
                    hidden_T(j)
                with nc.tensor.If(following[2] == 1):
                    up(j + 1, following[0])
                    if last:
                        pe.wait_ge(s_xelo, TILES)
                    else:
                        rows_T(j + 2)
                return following

            rows_T(0)
            pe.wait_ge(s_ew, 2)
            pe.wait_ge(s_xelo, 1)
            up_from(0, 0)
            rows_T(1)
            hidden_T(0)
            pe.wait_ge(s_te, 1)
            up(1, plan_of(nc.tensor, 1)[0])
            rows_T(2)
            with pe.Fori(0, (TILES - 3) // TURN) as i:
                plan = plan_of(nc.tensor, i * TURN + 1)
                for u in range(TURN):
                    plan = middle(i * TURN + u + 1, plan)
            plan = middle(TILES - 2, plan_of(nc.tensor, TILES - 2), last=True)
            outputs_before(TILES - 1, plan)
            with nc.tensor.If(plan[2] == 1):
                hidden_T(TILES - 1)
            with nc.tensor.If(plan_of(nc.tensor, TILES)[2] == 2):
                down(TILES - 1, E - 1)
                pe.wait_ge(s_he, 2 * TILES)


_INS = ['x', 'adj', 'L0_gnn_W1', 'L0_gnn_b1', 'L0_gnn_W3', 'L0_gnn_b3', 'L0_gnn_Wf', 'L0_gnn_bf', 'L0_ffn_gate_w',
        'L0_ffn_W1', 'L0_ffn_W2', 'L0_ffn_W3']


def kernel(**inputs):
    import numpy as np
    import concourse.bacc as bacc
    from concourse.bass_utils import run_bass_kernel_spmd

    nc = bacc.Bacc("TRN2", target_bir_lowering=False, num_devices=1)
    arrays, args = {}, []
    for name in _INS:
        a = np.ascontiguousarray(inputs[name])
        arrays[f"in_{name}"] = a
        args.append(nc.dram_tensor(f"in_{name}", a.shape, mybir.dt.from_np(a.dtype), kind="ExternalInput").ap())
    n, d = inputs['x'].shape
    o = nc.dram_tensor("out_0", (n + nc.NUM_PARTITIONS, d), F32, kind="ExternalOutput").ap()
    gnn_and_routed_ffn(nc, *args, o)
    r = run_bass_kernel_spmd(nc, [arrays], core_ids=[0])
    return r.results[0]["out_0"][:n]
```
